# Optimizing a Trainium2 kernel written in Bass

```python
import numpy as np
import jax
import jax.numpy as jnp

def _softmax(x, axis=-1):
    return jax.nn.softmax(x, axis=axis)

def _gelu(x):
    return jax.nn.gelu(x, approximate=True)

def _silu(x):
    return jax.nn.silu(x)

def _sigmoid(x):
    return jax.nn.sigmoid(x)

def _layernorm(x, axis=-1, eps=1e-05):
    m = jnp.mean(x, axis=axis, keepdims=True)
    v = jnp.var(x, axis=axis, keepdims=True)
    return (x - m) / jnp.sqrt(v + eps)

def _scatter_add(tgt, idx, src, axis=0):
    return tgt.at[idx].add(src)

def _segment_sum(src, seg, n):
    return jax.ops.segment_sum(src, seg, n)
kernel_name = 'mk_xattn_ffn_d2_seqx_r4_1ce000'

def setup_inputs(seed: int=0):
    np.random.seed(seed)
    _w = jnp.asarray

    def _rec_inputs():
        import jax
        import jax.numpy as jnp
        _rk = jax.random.key(seed)
        x = -0.0002928 + 1 * jax.random.normal(jax.random.fold_in(_rk, 1), (16, 128, 256), jnp.float32)
        _lenS = 128 - jax.random.randint(jax.random.fold_in(_rk, 7), (16,), 0, max(1, 128 // 4) + 1, jnp.int32)
        _lenS2 = 128 - jax.random.randint(jax.random.fold_in(_rk, 8), (16,), 0, max(1, 128 // 4) + 1, jnp.int32)
        _ctx_1024P = jax.random.normal(jax.random.fold_in(_rk, 11), (16, 16, 256), jnp.float32)
        _ctx_1024c = jax.random.dirichlet(jax.random.fold_in(_rk, 511), 0.3 * jnp.ones((16,), jnp.float32), (16, 128))
        _ctx_1024t = jnp.einsum('bsk,bkd->bsd', _ctx_1024c, _ctx_1024P)
        _ctx_1024t = _ctx_1024t * jax.lax.rsqrt(jnp.mean(jnp.square(_ctx_1024t)) + 1e-12) * 0.953939
        ctx_1024 = -1.39393e-06 + 0.999914 * (_ctx_1024t + 0.3 * jax.random.normal(jax.random.fold_in(_rk, 611), (16, 128, 256), jnp.float32))
        return (x, ctx_1024)
    x, ctx_1024 = _rec_inputs()

    def _L0_xattn_setup():
        import jax, jax.numpy as jnp
        import numpy as np
        B, S, H, NH = (2, 512, 256, 4)
        DH = H // NH
        EPS = 1e-06

        def _parallel_stabilized(qh, kh, vh, ig, fg):
            log_fg = jax.nn.log_sigmoid(fg)
            cs = jnp.cumsum(log_fg, axis=2)
            ltr = jnp.tril(jnp.ones((qh.shape[2], qh.shape[2]), dtype=bool))
            log_fg_mat = jnp.where(ltr, cs - jnp.swapaxes(cs, 2, 3), -jnp.inf)
            log_D = log_fg_mat + jnp.swapaxes(ig, 2, 3)
            max_log_D = jnp.max(log_D, axis=-1, keepdims=True)
            D = jnp.exp(log_D - max_log_D)
            qk = jnp.einsum('bhsd,bhtd->bhst', qh, kh) / jnp.sqrt(jnp.float32(DH))
            C = qk * D
            normalizer = jnp.maximum(jnp.abs(jnp.sum(C, axis=-1, keepdims=True)), jnp.exp(-max_log_D))
            return jnp.einsum('bhst,bhtd->bhsd', C / (normalizer + EPS), vh)
        key = jax.random.key(seed)
        ks = jax.random.split(key, 6)
        q = jax.random.normal(ks[0], (B, S, H), dtype=jnp.float32)
        k = jax.random.normal(ks[1], (B, S, H), dtype=jnp.float32)
        v = jax.random.normal(ks[2], (B, S, H), dtype=jnp.float32)
        igate_kernel = jax.random.normal(ks[3], (3 * H, NH), dtype=jnp.float32) * 0.02
        fgate_kernel = jax.random.normal(ks[4], (3 * H, NH), dtype=jnp.float32) * 0.02
        igate_bias = jax.random.normal(ks[5], (NH,), dtype=jnp.float32) * 0.1
        fgate_bias = jnp.linspace(3.0, 6.0, NH, dtype=jnp.float32)
        outnorm_scale = jnp.ones((H,), dtype=jnp.float32)
        return {'q': q, 'k': k, 'v': v, 'igate_kernel': igate_kernel, 'igate_bias': igate_bias, 'fgate_kernel': fgate_kernel, 'fgate_bias': fgate_bias, 'outnorm_scale': outnorm_scale}
    _L0_xattn_all = _L0_xattn_setup()
    _L0_xattn_in = {k: v for k, v in _L0_xattn_all.items() if k in ('igate_kernel', 'igate_bias', 'fgate_kernel', 'fgate_bias', 'outnorm_scale')}
    del _L0_xattn_all

    def _L0_ffn_setup():
        import jax, jax.numpy as jnp
        import numpy as np
        BLOCK = 32
        W_BITS = 4
        ACT_BITS = 16

        def act_qdq(x):
            qmax = 2.0 ** (ACT_BITS - 1) - 1.0
            scale = jnp.maximum(jnp.max(jnp.abs(x)) / qmax, 1e-12)
            return jnp.clip(jnp.round(x / scale), -qmax - 1.0, qmax) * scale

        def fixed_qdq_u16(x):
            scale = 1.0 / 65536.0
            return jnp.clip(jnp.round(x / scale), 0.0, 65535.0) * scale

        def lpbq_dequant(w):
            O, I = w.shape
            qmax = 2.0 ** (W_BITS - 1) - 1.0
            wb = w.reshape(O, I // BLOCK, BLOCK)
            s = jnp.maximum(jnp.max(jnp.abs(wb), axis=-1, keepdims=True) / qmax, 1e-12)
            wq = jnp.clip(jnp.round(wb / s), -qmax - 1.0, qmax) * s
            return wq.reshape(O, I)
        key = jax.random.key(seed)
        k1, k2, k3, k4 = jax.random.split(key, 4)
        B, S, H, I = (2, 1024, 256, 768)
        x = jax.random.normal(k1, (B, S, H), jnp.float32)
        w_gate = jax.random.normal(k2, (I, H), jnp.float32) * 0.02
        w_up = jax.random.normal(k3, (I, H), jnp.float32) * 0.02
        w_down = jax.random.normal(k4, (H, I), jnp.float32) * 0.02
        return {'x': x, 'w_gate': w_gate, 'w_up': w_up, 'w_down': w_down}
    _L0_ffn_all = _L0_ffn_setup()
    _L0_ffn_in = {k: v for k, v in _L0_ffn_all.items() if k in ('w_gate', 'w_up', 'w_down')}
    del _L0_ffn_all

    def _L1_xattn_setup():
        import jax, jax.numpy as jnp
        import numpy as np
        D_MODEL = 256
        N_HEADS = 16
        D_K = D_MODEL // N_HEADS
        key = jax.random.key(seed)
        ks = jax.random.split(key, 11)
        B, S = (2, 512)
        scale = 1.0 / np.sqrt(D_MODEL)
        return {'query': jax.random.normal(ks[0], (B, S, D_MODEL), jnp.float32), 'key': jax.random.normal(ks[1], (B, S, D_MODEL), jnp.float32), 'value': jax.random.normal(ks[2], (B, S, D_MODEL), jnp.float32), 'w_q': jax.random.normal(ks[3], (D_MODEL, D_MODEL), jnp.float32) * scale, 'b_q': jnp.zeros((D_MODEL,), jnp.float32), 'w_k': jax.random.normal(ks[4], (D_MODEL, D_MODEL), jnp.float32) * scale, 'b_k': jnp.zeros((D_MODEL,), jnp.float32), 'w_v': jax.random.normal(ks[5], (D_MODEL, D_MODEL), jnp.float32) * scale, 'b_v': jnp.zeros((D_MODEL,), jnp.float32), 'w_o': jax.random.normal(ks[6], (D_MODEL, D_MODEL), jnp.float32) * scale, 'b_o': jnp.zeros((D_MODEL,), jnp.float32)}
    _L1_xattn_all = _L1_xattn_setup()
    _L1_xattn_in = {k: v for k, v in _L1_xattn_all.items() if k in ('w_q', 'b_q', 'w_k', 'b_k', 'w_v', 'b_v', 'w_o', 'b_o')}
    del _L1_xattn_all

    def _L1_ffn_setup():
        import jax, jax.numpy as jnp
        import numpy as np
        NUM_GROUPS = 2
        EXPERT_CAPACITY = 160
        NUM_SELECTED = 2
        key = jax.random.key(seed)
        k1, k2, k3, k4 = jax.random.split(key, 4)
        B, S, H, E, F = (4, 512, 256, 8, 1024)
        return {'input_emb': jax.random.normal(k1, (B, S, H), dtype=jnp.float32), 'w_router': jax.random.normal(k2, (H, E), dtype=jnp.float32) * 0.02, 'wi': jax.random.normal(k3, (E, H, F), dtype=jnp.float32) * 0.02, 'wo': jax.random.normal(k4, (E, F, H), dtype=jnp.float32) * 0.02}
    _L1_ffn_all = _L1_ffn_setup()
    _L1_ffn_in = {k: v for k, v in _L1_ffn_all.items() if k in ('w_router', 'wi', 'wo')}
    del _L1_ffn_all
    return {'x': x, 'ctx_1024': ctx_1024, 'L0_xattn_igate_kernel': _L0_xattn_in['igate_kernel'], 'L0_xattn_igate_bias': _L0_xattn_in['igate_bias'], 'L0_xattn_fgate_kernel': _L0_xattn_in['fgate_kernel'], 'L0_xattn_fgate_bias': _L0_xattn_in['fgate_bias'], 'L0_xattn_outnorm_scale': _L0_xattn_in['outnorm_scale'], 'L0_ffn_w_gate': _L0_ffn_in['w_gate'], 'L0_ffn_w_up': _L0_ffn_in['w_up'], 'L0_ffn_w_down': _L0_ffn_in['w_down'], 'L1_xattn_w_q': _L1_xattn_in['w_q'], 'L1_xattn_b_q': _L1_xattn_in['b_q'], 'L1_xattn_w_k': _L1_xattn_in['w_k'], 'L1_xattn_b_k': _L1_xattn_in['b_k'], 'L1_xattn_w_v': _L1_xattn_in['w_v'], 'L1_xattn_b_v': _L1_xattn_in['b_v'], 'L1_xattn_w_o': _L1_xattn_in['w_o'], 'L1_xattn_b_o': _L1_xattn_in['b_o'], 'L1_ffn_w_router': _L1_ffn_in['w_router'], 'L1_ffn_wi': _L1_ffn_in['wi'], 'L1_ffn_wo': _L1_ffn_in['wo']}

def reference(x, ctx_1024, L0_xattn_igate_kernel, L0_xattn_igate_bias, L0_xattn_fgate_kernel, L0_xattn_fgate_bias, L0_xattn_outnorm_scale, L0_ffn_w_gate, L0_ffn_w_up, L0_ffn_w_down, L1_xattn_w_q, L1_xattn_b_q, L1_xattn_w_k, L1_xattn_b_k, L1_xattn_w_v, L1_xattn_b_v, L1_xattn_w_o, L1_xattn_b_o, L1_ffn_w_router, L1_ffn_wi, L1_ffn_wo):
    import jax
    import jax.numpy as jnp

    def _L0_xattn_ref(q, k, v, igate_kernel, igate_bias, fgate_kernel, fgate_bias, outnorm_scale):
        import jax, jax.numpy as jnp
        import numpy as np
        B, S, H, NH = (2, 512, 256, 4)
        DH = H // NH
        EPS = 1e-06

        def _parallel_stabilized(qh, kh, vh, ig, fg):
            log_fg = jax.nn.log_sigmoid(fg)
            cs = jnp.cumsum(log_fg, axis=2)
            ltr = jnp.tril(jnp.ones((qh.shape[2], qh.shape[2]), dtype=bool))
            log_fg_mat = jnp.where(ltr, cs - jnp.swapaxes(cs, 2, 3), -jnp.inf)
            log_D = log_fg_mat + jnp.swapaxes(ig, 2, 3)
            max_log_D = jnp.max(log_D, axis=-1, keepdims=True)
            D = jnp.exp(log_D - max_log_D)
            qk = jnp.einsum('bhsd,bhtd->bhst', qh, kh) / jnp.sqrt(jnp.float32(DH))
            C = qk * D
            normalizer = jnp.maximum(jnp.abs(jnp.sum(C, axis=-1, keepdims=True)), jnp.exp(-max_log_D))
            return jnp.einsum('bhst,bhtd->bhsd', C / (normalizer + EPS), vh)
        Bq, Sq, Hq = q.shape
        x = jnp.concatenate([q, k, v], axis=-1)
        ig = x @ igate_kernel + igate_bias
        fg = x @ fgate_kernel + fgate_bias
        ig = jnp.transpose(ig, (0, 2, 1))[..., None]
        fg = jnp.transpose(fg, (0, 2, 1))[..., None]
        qh = jnp.transpose(q.reshape(Bq, Sq, NH, DH), (0, 2, 1, 3))
        kh = jnp.transpose(k.reshape(Bq, Sq, NH, DH), (0, 2, 1, 3))
        vh = jnp.transpose(v.reshape(Bq, Sq, NH, DH), (0, 2, 1, 3))
        h = _parallel_stabilized(qh, kh, vh, ig, fg)
        mean = jnp.mean(h, axis=-1, keepdims=True)
        var = jnp.mean((h - mean) ** 2, axis=-1, keepdims=True)
        h_norm = (h - mean) * jax.lax.rsqrt(var + 1e-05)
        h_norm = h_norm * outnorm_scale.reshape(1, NH, 1, DH)
        out = jnp.transpose(h_norm, (0, 2, 1, 3)).reshape(Bq, Sq, Hq)
        return out

    def _L0_ffn_ref(x, w_gate, w_up, w_down):
        import jax, jax.numpy as jnp
        import numpy as np
        BLOCK = 32
        W_BITS = 4
        ACT_BITS = 16

        def act_qdq(x):
            qmax = 2.0 ** (ACT_BITS - 1) - 1.0
            scale = jnp.maximum(jnp.max(jnp.abs(x)) / qmax, 1e-12)
            return jnp.clip(jnp.round(x / scale), -qmax - 1.0, qmax) * scale

        def fixed_qdq_u16(x):
            scale = 1.0 / 65536.0
            return jnp.clip(jnp.round(x / scale), 0.0, 65535.0) * scale

        def lpbq_dequant(w):
            O, I = w.shape
            qmax = 2.0 ** (W_BITS - 1) - 1.0
            wb = w.reshape(O, I // BLOCK, BLOCK)
            s = jnp.maximum(jnp.max(jnp.abs(wb), axis=-1, keepdims=True) / qmax, 1e-12)
            wq = jnp.clip(jnp.round(wb / s), -qmax - 1.0, qmax) * s
            return wq.reshape(O, I)
        x = act_qdq(x)
        up = act_qdq(x @ lpbq_dequant(w_up).T)
        gate = act_qdq(x @ lpbq_dequant(w_gate).T)
        sig = fixed_qdq_u16(jax.nn.sigmoid(gate))
        gate = act_qdq(gate * sig)
        o = act_qdq(gate * up)
        return o @ lpbq_dequant(w_down).T

    def _L1_xattn_ref(query, key, value, w_q, b_q, w_k, b_k, w_v, b_v, w_o, b_o):
        import jax, jax.numpy as jnp
        import numpy as np
        D_MODEL = 256
        N_HEADS = 16
        D_K = D_MODEL // N_HEADS
        B, S, _ = query.shape

        def proj(x, w, b):
            y = jnp.einsum('bsd,ed->bse', x, w) + b
            return y.reshape(B, -1, N_HEADS, D_K).transpose(0, 2, 1, 3)
        q = proj(query, w_q, b_q)
        k = proj(key, w_k, b_k)
        v = proj(value, w_v, b_v)
        scores = jnp.einsum('bhqd,bhkd->bhqk', q, k) / np.sqrt(D_K)
        attn = jax.nn.softmax(scores, axis=-1)
        out = jnp.einsum('bhqk,bhkd->bhqd', attn, v)
        out = out.transpose(0, 2, 1, 3).reshape(B, S, D_MODEL)
        out = jnp.einsum('bsd,ed->bse', out, w_o) + b_o
        return out

    def _L1_ffn_ref(input_emb, w_router, wi, wo):
        import jax, jax.numpy as jnp
        import numpy as np
        NUM_GROUPS = 2
        EXPERT_CAPACITY = 160
        NUM_SELECTED = 2
        B, S, H = input_emb.shape
        E = w_router.shape[1]
        G = NUM_GROUPS
        T = B * S // G
        C = EXPERT_CAPACITY
        K = NUM_SELECTED
        x = input_emb.reshape(G, T, H)
        router_logits = jnp.einsum('gth,he->gte', x.astype(jnp.float32), w_router.astype(jnp.float32))
        router_probs = jax.nn.softmax(router_logits, axis=-1)
        gate, idx = jax.lax.top_k(router_probs, K)
        mask = jax.nn.one_hot(idx, E, dtype=jnp.float32)
        mask_kt = jnp.swapaxes(mask, 1, 2).reshape(G, K * T, E)
        pos = jnp.cumsum(mask_kt, axis=1) * mask_kt - 1.0
        pos = jnp.swapaxes(pos.reshape(G, K, T, E), 1, 2)
        disp_k = jax.nn.one_hot(pos, C, dtype=jnp.float32) * mask[..., None]
        dispatch = disp_k.sum(axis=2)
        combine = jnp.einsum('gtk,gtkec->gtec', gate, disp_k)
        expert_in = jnp.einsum('gtec,gth->egch', dispatch, x)
        h = jax.nn.relu(jnp.einsum('egch,ehf->egcf', expert_in, wi))
        expert_out = jnp.einsum('egcf,efh->egch', h, wo)
        y = jnp.einsum('gtec,egch->gth', combine, expert_out)
        return y.reshape(B, S, H)
    x = x + _L0_xattn_ref(_layernorm(x, axis=-1), ctx_1024, ctx_1024, L0_xattn_igate_kernel, L0_xattn_igate_bias, L0_xattn_fgate_kernel, L0_xattn_fgate_bias, L0_xattn_outnorm_scale)
    x = x + _L0_ffn_ref(_layernorm(x, axis=-1), L0_ffn_w_gate, L0_ffn_w_up, L0_ffn_w_down)
    x = x + _L1_xattn_ref(_layernorm(x, axis=-1), ctx_1024, ctx_1024, L1_xattn_w_q, L1_xattn_b_q, L1_xattn_w_k, L1_xattn_b_k, L1_xattn_w_v, L1_xattn_b_v, L1_xattn_w_o, L1_xattn_b_o)
    x = x + _L1_ffn_ref(_layernorm(x, axis=-1), L1_ffn_w_router, L1_ffn_wi, L1_ffn_wo)
    return x

_drawn_inputs = setup_inputs


def setup_inputs(seed=0):
    import zlib

    import numpy as np

    out = dict(_drawn_inputs(seed))
    spreads = {'L0_xattn_outnorm_scale': (1.0, 0.2),
     'L1_xattn_b_q': (0.0, 0.601),
     'L1_xattn_b_k': (0.0, 0.8),
     'L1_xattn_b_v': (0.0, 0.1),
     'L1_xattn_b_o': (0.0, 0.1)}
    factors = {'L0_xattn_igate_bias': 8.0,
     'L0_ffn_w_gate': 3.106,
     'L0_ffn_w_up': 2.912,
     'L0_ffn_w_down': 2.904,
     'L1_ffn_w_router': 3.688,
     'L1_ffn_wi': 3.978,
     'L1_ffn_wo': 3.319}
    for name, (base, spread) in spreads.items():
        noise = np.random.default_rng([zlib.crc32(name.encode()), seed]).standard_normal(out[name].shape)
        drawn = base * np.exp(spread * noise) if base else spread * noise
        out[name] = jnp.asarray(drawn.astype(out[name].dtype))
    for name, factor in factors.items():
        out[name] = (out[name] * factor).astype(out[name].dtype)
    return out
```

```python
from contextlib import ExitStack

import numpy as np
import concourse.bass as bass
from concourse import mybir

F32 = mybir.dt.float32
BF16 = mybir.dt.bfloat16
I32 = mybir.dt.int32
U32 = mybir.dt.uint32
ALU = mybir.AluOpType
ACT = mybir.ActivationFunctionType
AX = mybir.AxisListType

P = 128
ROUND = 12582912.0
QMAX = 32767.0
TINY = 1e-12
EPS = 1e-5


def steps(eng, n, stages):
    deepest = max(lag for _, lag in stages)
    total = n + deepest
    first = deepest + 2
    turns = max(0, (n - first) // 2)
    if turns < 2:
        turns = 0

    def one(s):
        for fn, lag in stages:
            b = s - lag
            if 0 <= b < n:
                fn(b, b % 2, b // 2)

    last = first + 2 * turns if turns else first
    for s in range(first):
        one(s)
    if turns:
        with eng.Fori(0, turns) as i:
            for d in range(2):
                for fn, lag in stages:
                    b = first + d - lag
                    fn(2 * i + b, b % 2, i + b // 2)
    for s in range(last, total):
        one(s)


def at(t, b):
    if isinstance(b, int):
        return t[:, b]
    ap = t[:, bass.ds(b, 1)]
    return ap.squeeze(1)


def cols(b, n):
    return bass.ds(b * n, n)


def free_after(eng, sem, b, per=1):
    if isinstance(b, int) and b < 2:
        return
    eng.wait_ge(sem, (b - 1) * per)


def build(nc, A, out):
    x_d = A["x"].rearrange("b s d -> s b d")
    ctx_d = A["ctx_1024"].rearrange("b s d -> s b d")
    NB, S, D = A["x"].shape
    KD = D // P
    NH0 = A["L0_xattn_igate_bias"].shape[0]
    DH0 = D // NH0
    FF = A["L0_ffn_w_gate"].shape[0]
    FT = FF // P
    DH1, NH1 = 16, D // 16
    NE = A["L1_ffn_w_router"].shape[1]
    NF = A["L1_ffn_wi"].shape[2]
    NFT = NF // P
    NG, CAP, TOPK = 2, 160, 2
    TG = NB // NG
    ROWS = NG * CAP
    SPARE = CAP - P
    SELW = P + NG * SPARE
    BLK = 32
    assert S == P and NB == 16 and D == 256

    ctx = ExitStack()
    with ctx:
        def sb(name, shape, dt=F32):
            return ctx.enter_context(nc.sbuf_tensor(name, shape, dt))

        def sem(name):
            return ctx.enter_context(nc.semaphore(name))

        RW = D + NE
        xr_d = nc.dram_tensor("token_rows", (NB * S, RW), F32, kind="Internal").ap()
        out_rows = out.rearrange("b s d -> (b s) d")

        ident = sb("ident", [P, P])
        ones = sb("ones", [P, P])
        tri = sb("tri", [P, P])
        stri = sb("stri", [P, P], BF16)
        onesb = sb("onesb", [P, P], BF16)
        cidx = sb("cidx", [P, SELW], BF16)
        ids = sb("ids", [P, NB, 2], BF16)
        pidx = sb("pidx", [P, 2], I32)
        par = sb("par", [P, 2])
        gb = sb("gb", [P, 2 * NH0])
        oscale = sb("oscale", [P, D])
        bv = sb("bv", [P, D])
        bo = sb("bo", [P, D])
        bq = sb("bq", [P, KD])
        bk = sb("bk", [P, KD])
        wgate_g = sb("wgate_g", [P, 6, 2 * NH0])
        wrt = sb("wrt", [P, KD, NE])
        wT = [sb(f"wT{n}", [P, KD, D]) for n in range(4)]
        wupT = sb("wupT", [P, KD, FF])
        wgtT = sb("wgtT", [P, KD, FF])
        wdnT = sb("wdnT", [P, FT, D])
        X = sb("X", [P, NB, D])
        XIT = sb("XIT", [P, KD * NB * S])
        KT = sb("KT", [P, KD, NB * S])
        V = sb("V", [P, NB, NH1, DH1 + 1])
        T = sb("T", [P, 2, D])
        XCT = sb("XCT", [P, 2, 4, P])
        Cu = sb("Cu", [P, 2, D])
        arena = sb("arena", [P, 2 * FT * NB * S])

        def view(o, *shape):
            n = int(np.prod(shape))
            names = "abcd"[:len(shape)]
            ap = arena[:, o:o + n]
            if len(shape) == 1:
                return ap
            kw = {names[k]: shape[k] for k in range(1, len(shape))}
            return ap.rearrange(f"p ({' '.join(names)}) -> p {' '.join(names)}", **kw)

        HALF = FT * NB * S
        U = view(0, FT, NB * S)
        G = view(HALF, FT, NB * S)
        HU = view(0, NB, NH0, DH0 + 1)
        H = view(4160, NB * NH0, DH0)
        HD = view(8256, 2, NH0, P)
        HC = view(9280, 2, NH0, P)
        VU = view(11440, 2, NH0, DH0 + 1)
        XL = view(0, NB, D)
        CX = view(HALF, NB, D)
        WN = view(HALF + 4096, 3, 1536)
        LN = view(HALF + 4096 + 4608, 4, KD, D)
        SG = KT[:, 0, 0:2 * FT * P].rearrange("p (u f n) -> p u f n", u=2, f=FT)
        OT = XIT[:, 0:2 * FT * P].rearrange("p (u f n) -> p u f n", u=2, f=FT)
        XITv = XIT[:, :].rearrange("p (k n) -> p k n", k=KD)
        PR = view(0, 2, NH1, P)
        PT = view(4096, 2, NH1, P)
        KM = view(8192, 2, KD, 2, P)
        QT = view(9216, 2, KD, P)
        AO = view(9728, 2, D)
        AT = view(10240, 2, KD, P)
        HT = view(0, 2, NFT, ROWS)
        XE = view(5120, 2, 3, RW)
        XET = view(6704, 2, KD, ROWS)
        YG = view(7984, 3, D)
        SEL = view(8752, 2 * NB * SELW // 2).bitcast(BF16).rearrange("p (u b c) -> p u b c", u=2, b=NB)
        XR = view(12160, NB, RW)
        WI = view(16384, 2, KD, NF)
        WO = view(20480, 2, NFT, D)

        ST = sb("ST", [P, NB * NH0, 6])
        mean = sb("mean", [P, NB * NH0])
        rstd = sb("rstd", [P, NB * NH0])
        s1 = sb("s1", [P, NB * NH0])
        s2 = sb("s2", [P, NB * NH0])
        s3 = sb("s3", [P, NB * NH0])
        var = sb("var", [P, NB * NH0])
        lnv = sb("lnv", [P, NB * NH0])
        yv = sb("yv", [P, NB * NH0])
        GA = sb("GA", [P, NB, 2 * NH0])
        AG = sb("AG", [P, NB, 2 * NH0])
        MAu = sb("MAu", [P, 2, 2 * NH0])
        lf = view(11120, NB, NH0)
        az = view(11184, NB, NH0)
        ez = view(11248, NB, NH0)
        Acol = view(11312, NB, NH0)
        aT = view(10736, P)[0:NB * NH0]
        mT = view(10864, P)[0:NB * NH0]
        zT = view(10992, P)[0:NB * NH0]
        nm = sb("nm", [P, NB, NH0])
        nmx = view(11376, NB, NH0)
        den = sb("den", [P, 2, 2, NH0])
        am = sb("am", [P, 2, 24])
        gm = sb("gm", [P, 2])
        gr = sb("gr", [2, 2])
        gd = sb("gd", [2, 2])
        sc = sb("sc", [P, 24])
        wam, wsc, winv = (view(10304 + 144 * n, 3, 48) for n in range(3))
        rm = sb("rm", [P, 2, NH1])
        rs = sb("rs", [P, 2, NH1])
        LG = XR[:, :, D:]
        r1 = sb("r1", [P, NB])
        gates = sb("gates", [P, TOPK, NB])
        gcol = sb("gcol", [P, 2, 3])
        num = sb("num", [P, 2, 3])
        token = sb("token", [P, NE, 3], U32)
        RT = [XIT[:, 256 * n:256 * n + 256] for n in range(5)]
        OH, pos, tmp = (RT[n].rearrange("p (k b e) -> p k b e", k=TOPK, b=NB) for n in (0, 1, 2))
        tot, inc = (RT[n].rearrange("p (g e k t) -> p g e k t", g=NG, e=NE, k=TOPK) for n in (3, 4))
        q1 = XIT[:, 1280:1408].rearrange("p (b e) -> p b e", b=NB)
        rank8 = XIT[:, 1408:1536].rearrange("p (b e) -> p b e", b=NB)
        place = XIT[:, 1536:1664].rearrange("p (b e) -> p b e", b=NB)
        shift = XIT[:, 1664:1792].rearrange("p (b e) -> p b e", b=NB)
        segm = XIT[:, 1792:2048]
        OHb = XIT[:, 2048:2176].bitcast(BF16)
        placeb = XIT[:, 2176:2240].bitcast(BF16).rearrange("p (b e) -> p b e", b=NB)
        LW = XIT[:, 2240:2368].rearrange("p (b e) -> p b e", b=NB)
        cidx_f = XIT[:, 2368:2368 + SELW]
        ids_f = XIT[:, 2560:2560 + 2 * NB].rearrange("p (b c) -> p b c", b=NB)

        pA = ctx.enter_context(nc.psum_tensor("pA", [P, 4, 512], F32))
        pB = ctx.enter_context(nc.psum_tensor("pB", [P, 2, 512], F32))
        pC = ctx.enter_context(nc.psum_tensor("pC", [P, 2, 512], F32))
        ps = [pA[:, i, :] for i in range(4)] + [pB[:, i, :] for i in range(2)] + [pC[:, i, :] for i in range(2)]
        S_ = {}

        class Sems:

            def __getitem__(self, name):
                if name not in S_:
                    S_[name] = sem(name)
                return S_[name]

        s = Sems()
        block = ctx.enter_context(nc.Block())

        def chain(eng, name):
            count = [0]

            def link(ins):
                count[0] += 1
                ins.then_inc(s[name], 1)
                eng.wait_ge(s[name], count[0])
            return link

        XQ = 4
        WB = 3 * 48 // NB

        def W_b(b):
            return WN[:, :, :].rearrange("p m (k c) -> p (m k) c", c=BLK)[:, cols(b, WB), :]

        def S_b(t, b):
            return t[:, :, :].rearrange("p m k -> p (m k)")[:, cols(b, WB)]

        def H_b(b):
            return H[:, cols(b, NH0), :].rearrange("p h d -> p (h d)")

        def F_b(t, b):
            return t[:, :, cols(b, P)]

        @block.sync
        def _(sp):
            def bcast(dst, src):
                sp.dma_start(dst, src.partition_broadcast(P)).then_inc(s["small_in"], 16)

            def late(dst, src):
                sp.dma_start(dst, src.partition_broadcast(P)).then_inc(s["late_in"], 16)

            def quarter(dst, src, q, name):
                sp.dma_start(dst[:, 4 * q:4 * q + 4, :], src[:, 4 * q:4 * q + 4, :]).then_inc(s[name], 16)
            for q in range(XQ):
                quarter(X, x_d, q, f"x_in{q}")
            gk = wgate_g
            sp.dma_start(gk[:, :, 0:NH0], A["L0_xattn_igate_kernel"].rearrange("(k p) h -> p k h", p=P)).then_inc(s["small_in"], 16)
            sp.dma_start(gk[:, :, NH0:], A["L0_xattn_fgate_kernel"].rearrange("(k p) h -> p k h", p=P)).then_inc(s["small_in"], 16)
            bcast(gb[:, 0:NH0], A["L0_xattn_igate_bias"])
            bcast(gb[:, NH0:], A["L0_xattn_fgate_bias"])
            quarter(CX, ctx_d, 0, "c_in")
            sp.dma_start(WN[:, 0, :].rearrange("p (t d) -> p t d", t=FT), A["L0_ffn_w_up"].rearrange("(t p) d -> p t d", p=P)).then_inc(s["wbig_in"], 16)
            quarter(CX, ctx_d, 1, "c_in")
            sp.dma_start(WN[:, 1, :].rearrange("p (t d) -> p t d", t=FT), A["L0_ffn_w_gate"].rearrange("(t p) d -> p t d", p=P)).then_inc(s["wbig_in"], 16)
            quarter(CX, ctx_d, 2, "c_in")
            sp.dma_start(WN[:, 2, :].rearrange("p (t d) -> p t d", t=KD), A["L0_ffn_w_down"].rearrange("(t p) d -> p t d", p=P)).then_inc(s["wbig_in"], 16)
            quarter(CX, ctx_d, 3, "c_in")
            late(oscale[:, :], A["L0_xattn_outnorm_scale"])
            late(bv[:, :], A["L1_xattn_b_v"])
            late(bo[:, :], A["L1_xattn_b_o"])
            sp.dma_start(bk[:, :], A["L1_xattn_b_k"].rearrange("(k p) -> p k", p=P), allow_slow_non_contiguous=True).then_inc(s["late_in"], 16)
            sp.dma_start(bq[:, :], A["L1_xattn_b_q"].rearrange("(k p) -> p k", p=P), allow_slow_non_contiguous=True).then_inc(s["late_in"], 16)
            sp.dma_start(wrt[:, :, :], A["L1_ffn_w_router"].rearrange("(k p) e -> p k e", p=P)).then_inc(s["late_in"], 16)
            for n, nme in ((1, "k"), (2, "v"), (0, "q"), (3, "o")):
                sp.dma_start(LN[:, n], A[f"L1_xattn_w_{nme}"].rearrange("(k p) d -> p k d", p=P)).then_inc(s[f"w{nme}_in"], 16)


            def ctx_again(b, u, h):
                if isinstance(b, int) and b < 2:
                    sp.wait_ge(s["tr2_done"], NB)
                free_after(sp, s["tr4_done"], b)
                sp.dma_start(Cu[:, u, :], at(ctx_d, b)).then_inc(s[f"ctx_in{u}"], 16)
            steps(sp, NB, [(ctx_again, 0)])

            def weights_in(e, u, h):
                if isinstance(e, int) and e < 2:
                    sp.wait_ge(s["gm_ready"], 4)
                free_after(sp, s["h_done"], e, NFT)
                sp.dma_start(WI[:, u], A["L1_ffn_wi"][bass.ds(e, 1)].squeeze(0).rearrange("(k p) f -> p k f", p=P)).then_inc(s[f"wi_in{u}"], 16)

            def weights_out(e, u, h):
                free_after(sp, s["ec_done"], e, 3)
                sp.dma_start(WO[:, u], A["L1_ffn_wo"][bass.ds(e, 1)].squeeze(0).rearrange("(k p) f -> p k f", p=P)).then_inc(s[f"wo_in{u}"], 16)
            weights_in(0, 0, 0)
            weights_out(0, 0, 0)
            weights_in(1, 1, 0)
            weights_out(1, 1, 0)
            for q in range(XQ):
                sp.wait_ge(s["x3_ready"], 4 * q + 4)
                sp.dma_start(out.rearrange("b s d -> s b d")[:, 4 * q:4 * q + 4, :], X[:, 4 * q:4 * q + 4, :]).then_inc(s["x3_out"], 16)
            xr = xr_d.rearrange("(b p) d -> p b d", p=P)
            for q in range(XQ):
                sp.wait_ge(s["xr_ready"], 4 * q + 4)
                sp.dma_start(xr[:, 4 * q:4 * q + 4, 0:D], XR[:, 4 * q:4 * q + 4, 0:D]).then_inc(s["xr_out"], 16)
            sp.wait_ge(s["probs"], 1)
            sp.dma_start(xr[:, :, D:], LG[:, :, :]).then_inc(s["xr_out"], 16)

            def both(e, u, h):
                if isinstance(e, int) and e < 2:
                    return
                weights_in(e, u, h)
                weights_out(e, u, h)
            steps(sp, NE, [(both, 0)])
            sp.wait_ge(s["rows_out"], 16 * 3 * NE)
            sp.wait_ge(s["x3_out"], 16 * XQ)

        @block.gpsimd
        def _(pool):
            link = chain(pool, "pool_chain")
            nc.gpsimd.memset(ones[:, :], 1.0)
            nc.gpsimd.memset(onesb[:, :], 1.0)
            nc.gpsimd.memset(zT[:, :], 0.0)
            nc.gpsimd.memset(V[:, :, :, DH1:], 1.0)
            nc.gpsimd.memset(VU[:, :, :, DH0:], 1.0)
            link(nc.gpsimd.memset(ident[:, :], 0.0))
            nc.gpsimd.affine_select(out=ident[:, :], in_=ident[:, :], compare_op=ALU.not_equal, fill=1.0,
                                    base=0, pattern=[[-1, P]], channel_multiplier=1)
            nc.gpsimd.affine_select(out=tri[:, :], in_=ones[:, :], compare_op=ALU.is_ge, fill=0.0,
                                    base=0, pattern=[[1, P]], channel_multiplier=-1)
            nc.gpsimd.affine_select(out=stri[:, :], in_=onesb[:, :], compare_op=ALU.is_gt, fill=0.0,
                                    base=0, pattern=[[1, P]], channel_multiplier=-1)
            nc.gpsimd.iota(pidx[:, 0:1], pattern=[[0, 1]], base=0, channel_multiplier=1).then_inc(s["consts"], 1)

            def w_scale(b, u, h):
                pool.wait_ge(s["w_step"], 5 * b + 5)
                nc.gpsimd.tensor_tensor(W_b(b), W_b(b), S_b(wsc, b).unsqueeze(2).broadcast_to([P, WB, BLK]), ALU.mult).then_inc(s["w_q"], 1)
            steps(pool, NB, [(w_scale, 0)])

            def causal(b, u, h):
                pool.wait_ge(s["c_ready"], b + 1)
                nc.gpsimd.tensor_tensor(HC[:, u], HC[:, u], tri[:, :].unsqueeze(1).broadcast_to([P, NH0, P]), ALU.mult).then_inc(s["c_masked"], 1)

            def copy_v(b, u, h):
                free_after(pool, s["av_done"], b)
                c = at(CX, b).rearrange("p (h d) -> p h d", h=NH0)
                nc.gpsimd.tensor_tensor(VU[:, u, :, 0:DH0], c, ones[:, 0:DH0].unsqueeze(1).broadcast_to([P, NH0, DH0]), ALU.mult).then_inc(s["v_copied"], 1)
            pool.wait_ge(s["c_in"], 16 * XQ)
            steps(pool, NB, [(copy_v, 0), (causal, 0)])
            pool.wait_ge(s["late_in"], 16 * 6)

            def h_scale(b, u, h):
                pool.wait_ge(s["h_normed"], b + 1)
                nc.gpsimd.tensor_tensor(H_b(b), H_b(b), oscale[:, :], ALU.mult).then_inc(s["h_scaled"], 1)
            steps(pool, NB, [(h_scale, 0)])

            def gate_sig(b, u, h):
                pool.wait_ge(s["sg_int"], b + 1)
                nc.gpsimd.tensor_tensor(F_b(G, b), F_b(G, b), SG[:, u], ALU.mult).then_inc(s["gs_done"], 1)
            steps(pool, NB, [(gate_sig, 0)])

            def v_bias(b, u, h):
                pool.wait_ge(s["kv_copied"], b + 1)
                v = at(V, b)[:, :, 0:DH1]
                nc.gpsimd.tensor_tensor(v, v, bv[:, :].rearrange("p (h d) -> p h d", h=NH1), ALU.add).then_inc(s["v_biased"], 1)
            steps(pool, NB, [(v_bias, 0)])

            def split_keys(b, u, h):
                if isinstance(b, int) and b == 0:
                    pool.wait_ge(s["down_done"], NB)
                free_after(pool, s["scores"], b)
                for r in range(2):
                    last = nc.gpsimd.tensor_tensor(KM[:, u, :, r, :], KT[:, :, cols(b, P)], par[:, r:r + 1].unsqueeze(2).broadcast_to([P, KD, P]), ALU.mult)
                last.then_inc(s["km_ready"], 1)

            def add_bo(b, u, h):
                pool.wait_ge(s["xn3"], b + 1)
                nc.gpsimd.tensor_tensor(at(X, b), at(X, b), bo[:, :], ALU.add).then_inc(s["bo_added"], 1)
            steps(pool, NB, [(split_keys, 0), (add_bo, 0)])

            nc.gpsimd.iota(rank8[:, :, :], pattern=[[0, NB], [-1, NE]], base=NE, channel_multiplier=0,
                           allow_small_or_imprecise_dtypes=True)
            nc.gpsimd.iota(cidx_f, pattern=[[1, SELW]], base=1, channel_multiplier=0, allow_small_or_imprecise_dtypes=True)
            nc.gpsimd.iota(ids_f[:, :, 0], pattern=[[P, NB]], base=-NB * P, channel_multiplier=0, allow_small_or_imprecise_dtypes=True)
            nc.gpsimd.iota(ids_f[:, :, 1], pattern=[[0, NB]], base=0, channel_multiplier=1, allow_small_or_imprecise_dtypes=True)
            pool.wait_ge(s["o_done"], NB)
            nc.gpsimd.memset(XE[:, :, :, :], 0.0)
            nc.gpsimd.memset(YG[:, :, :], 0.0)
            link(nc.gpsimd.iota(segm[:, :], pattern=[[0, NG * NE], [1, TOPK * TG]], base=0,
                                channel_multiplier=0, allow_small_or_imprecise_dtypes=True))
            nc.gpsimd.tensor_scalar(segm[:, :], segm[:, :], 1.0, None, ALU.min).then_inc(s["tables"], 1)

            def indirect(e, c, dram, sbuf, gather):
                n = P if c < 2 else ROWS - 2 * P
                where = bass.IndirectOffsetOnAxis(ap=token[0:n, e, c:c + 1], axis=0)
                if gather:
                    return nc.gpsimd.indirect_dma_start(out=sbuf[0:n, c, :], out_offset=None, in_=dram, in_offset=where,
                                                        bounds_check=NB * S - 1, oob_is_err=False)
                return nc.gpsimd.indirect_dma_start(out=dram, out_offset=where, in_=sbuf[0:n, c, :], in_offset=None,
                                                    bounds_check=NB * S - 1, oob_is_err=False)
            pool.wait_ge(s["xr_out"], 16 * (XQ + 1))
            pool.wait_ge(s["x3_out"], 16 * XQ)
            for t in range(NE + 3):
                if t < NE:
                    pool.wait_ge(s["token_ready"], t + 1)
                    if t >= 2:
                        pool.wait_ge(s["xe_tr"], t - 1)
                        pool.wait_ge(s["gcol_ready"], t - 1)
                    for c in range(3):
                        indirect(t, c, xr_d, XE[:, t % 2], True).then_inc(s[f"xe_in{t % 2}"], 16)
                e = t - 3
                if e >= 0:
                    if e >= 1:
                        pool.wait_ge(s["rows_out"], 16 * 3 * e)
                    for c in range(3):
                        indirect(e, c, out_rows, YG, True).then_inc(s["yg_in"], 16)
                    for c in range(3):
                        pool.wait_ge(s["y_ready"], 3 * e + c + 1)
                        indirect(e, c, out_rows, YG, False).then_inc(s["rows_out"], 16)

        @block.scalar
        def _(act):
            link = chain(act, "act_chain")

            def rsqrt(k, n):
                act.wait_ge(s["ln_var"], k + 1)
                link(nc.scalar.activation(lnv[:, 0:n], var[:, 0:n], ACT.Ln))
                nc.scalar.activation(yv[:, 0:n], lnv[:, 0:n], ACT.Exp, scale=-0.5).then_inc(s["ln_y"], 1)

            rsqrt(0, NB)

            def copy_t(b, u, h):
                act.wait_ge(s["tr_done"], b + 1)
                free_after(act, s["g_done"], b)
                nc.scalar.activation(XCT[:, u], ps[u][:, :].rearrange("p (k n) -> p k n", k=4), ACT.Copy).then_inc(s["xct_ready"], 1)

            steps(act, NB, [(copy_t, 0)])
            act.wait_ge(s["fgate_dve"], 1)
            link(nc.scalar.activation(ez[:, :, :], az[:, :, :], ACT.Exp, scale=-1.0))
            nc.scalar.activation(ez[:, :, :], ez[:, :, :], ACT.Ln, bias=1.0).then_inc(s["fgate_act"], 1)
            act.wait_ge(s["fgate_dve"], 5)
            nc.scalar.activation(nm[:, :, :], nmx[:, :, :], ACT.Exp, scale=-1.0).then_inc(s["fgate_act"], 1)

            def decay(b, u, h):
                act.wait_ge(s["mb_done"], b + 1)
                free_after(act, s["c_ready"], b)
                for n in range(NH0):
                    last = nc.scalar.activation(HD[:, u, 2 * (n % 2) + n // 2, :], ps[2 + u][:, n * P:(n + 1) * P], ACT.Exp,
                                                bias=MAu[:, u, NH0 + n:NH0 + n + 1], scale=-1.0)
                last.then_inc(s["decay"], 1)

            def copy_u(b, u, h):
                act.wait_ge(s["av_done"], b + 1)
                nc.scalar.activation(at(HU, b), pC[:, u, 0:NH0 * (DH0 + 1)].rearrange("p (h d) -> p h d", h=NH0), ACT.Copy).then_inc(s["u_copied"], 1)
            steps(act, NB, [(decay, 0), (copy_u, 2)])
            rsqrt(1, NB * NH0)
            for n in range(13):
                if n < 9:
                    dst = (wupT, wgtT)[n // 3][:, :, :].rearrange("p k (g c) -> p k g c", g=3)[:, :, n % 3, :] if n < 6 else \
                        wdnT[:, 2 * (n - 6):2 * (n - 6) + 2, :]
                else:
                    dst = wT[n - 9][:, :, :]
                act.wait_ge(s["wtr_done"], n + 1)
                nc.scalar.activation(dst, ps[2 + n % 2][:, :].rearrange("p (k c) -> p k c", k=2), ACT.Copy).then_inc(s["wtr_copied"], 1)
            rsqrt(2, NB)

            def copy_x(b, u, h):
                act.wait_ge(s["tr3_done"], b + 1)
                nc.scalar.activation(XITv[:, :, cols(b, P)], ps[u][:, 0:2 * P].rearrange("p (k n) -> p k n", k=2), ACT.Copy).then_inc(s["xit_ready"], 1)

            def evacuate(dst, name, c, f):
                act.wait_ge(s[f"{name}_done"], c * FT + f + 1)
                nc.scalar.activation(dst[:, f, cols(c, 512)], ps[2 + f][:, :], ACT.Copy).then_inc(s[f"{name}_out"], 1)

            def gate_chunk(c):
                for j in range(4):
                    copy_x(4 * c + j, j % 2, 0)
                for f in range(FT):
                    evacuate(G, "gate", c, f)
            gate_chunk(0)
            with act.Fori(1, 4) as c:
                gate_chunk(c)
            act.wait_ge(s["sc_gate"], 1)

            def up_chunk(c):
                for f in range(FT):
                    evacuate(U, "up", c, f)
                    if f >= 4:
                        continue
                    b, u = 4 * c + f, f % 2
                    act.wait_ge(s["g_int"], b + 1)
                    if not (isinstance(c, int) and c == 0 and f < 2):
                        act.wait_ge(s["gs_done"], b - 1)
                    nc.scalar.activation(SG[:, u], F_b(G, b), ACT.Sigmoid, scale=sc[:, 5:6]).then_inc(s["sig"], 1)
                    act.wait_ge(s["sig"], b + 1)
                    nc.scalar.activation(SG[:, u], SG[:, u], ACT.Copy, scale=65536.0, bias=ROUND).then_inc(s["sig_b"], 1)
            up_chunk(0)
            with act.Fori(1, 4) as c:
                up_chunk(c)
            act.wait_ge(s["sc_up"], 1)

            def up_int(b, u, h):
                nc.scalar.activation(F_b(U, b), F_b(U, b), ACT.Copy, scale=sc[:, 6:7], bias=ROUND).then_inc(s["u_b"], 1)

            def copy_c4(b, u, h):
                act.wait_ge(s["tr4_done"], b + 1)
                free_after(act, s["kv_done"], b)
                nc.scalar.activation(XCT[:, u, 2:4], ps[u][:, 0:2 * P].rearrange("p (k n) -> p k n", k=2), ACT.Copy).then_inc(s["xct4_ready"], 1)

            def keys_values(b, u, h):
                act.wait_ge(s["kv_done"], b + 1)
                for k in range(KD):
                    nc.scalar.activation(KT[:, k, cols(b, P)], ps[2 + u][:, k * P:(k + 1) * P], ACT.Identity, bias=bk[:, k:k + 1])
                nc.scalar.activation(at(V, b)[:, :, 0:DH1], ps[2 + u][:, 2 * P:4 * P].rearrange("p (h d) -> p h d", h=NH1), ACT.Copy).then_inc(s["kv_copied"], 1)
            act.wait_ge(s["late_in"], 16 * 6)
            steps(act, NB, [(copy_c4, 0), (up_int, 0), (keys_values, 1)])
            rsqrt(3, NB)

            def xt_copy(b, u, h):
                act.wait_ge(s["c_tr"], b + 1)
                free_after(act, s["c_q"], b)
                nc.scalar.activation(XCT[:, u, 0:2], ps[4][:, 0:2 * P].rearrange("p (k n) -> p k n", k=2), ACT.Copy).then_inc(s["c_xt"], 1)

            def q_out(b, u, h):
                act.wait_ge(s["c_q"], b + 1)
                free_after(act, s["scores"], b)
                for k in range(KD):
                    last = nc.scalar.activation(QT[:, u, k, :], ps[4][:, (2 + k) * P:(3 + k) * P], ACT.Identity, scale=0.25, bias=bq[:, k:k + 1])
                last.then_inc(s["qt_ready"], 1)

            def exps(b, u, h):
                act.wait_ge(s["s_sub"], b + 1)
                nc.scalar.activation(PR[:, u], PR[:, u], ACT.Exp).then_inc(s["p_ready"], 1)

            def pt_copy(b, u, groups):
                for g in groups:
                    act.wait_ge(s["pt_tr"], b * 4 + g + 1)
                    nc.scalar.activation(PT[:, u, 4 * g:4 * g + 4, :], pC[:, g % 2, :].rearrange("p (k n) -> p k n", k=4), ACT.Copy).then_inc(s["pt_ready"], 1)

            def pt_first(b, u, h):
                free_after(act, s["pv_done"], b)
                pt_copy(b, u, (0, 1))

            def pt_rest(b, u, h):
                pt_copy(b, u, (2, 3))

            def at_copy(b, u, h):
                act.wait_ge(s["a_tr"], b + 1)
                free_after(act, s["o_done"], b)
                nc.scalar.activation(AT[:, u], ps[4][:, 0:2 * P].rearrange("p (k n) -> p k n", k=2), ACT.Copy).then_inc(s["at_ready"], 1)
            steps(act, NB, [(exps, 2), (xt_copy, 0), (q_out, 0), (pt_first, 2), (at_copy, 3), (pt_rest, 2)])
            rsqrt(4, NB)

            def xt4(b, u, h):
                act.wait_ge(s["d_tr"], b + 1)
                free_after(act, s["d_lg"], b)
                nc.scalar.activation(XCT[:, u, 0:2], ps[u][:, 0:2 * P].rearrange("p (k n) -> p k n", k=2), ACT.Copy).then_inc(s["d_xt"], 1)
            steps(act, NB, [(xt4, 0)])
            act.wait_ge(s["lg_sub"], 1)
            nc.scalar.activation(LG[:, :, :], LG[:, :, :], ACT.Exp).then_inc(s["lg_exp"], 1)

            def xet(e, u, h):
                act.wait_ge(s["xe_tr"], e + 1)
                free_after(act, s["h_done"], e, NFT)
                for k in range(KD):
                    last = nc.scalar.activation(XET[:, u, k, :], ps[k][:, 0:ROWS], ACT.Copy)
                last.then_inc(s["xet_ready"], 1)

            def relu(e, u, h):
                free_after(act, s["ec_done"], e, 3)
                for f in range(NFT):
                    act.wait_ge(s["h_done"], e * NFT + f + 1)
                    nc.scalar.activation(HT[:, u, f, :], ps[2 + f % 2][:, 0:ROWS], ACT.Relu).then_inc(s["h_relu"], 1)
            steps(act, NE, [(relu, 1), (xet, 0)])

        @block.vector
        def _(dve):
            link = chain(dve, "dve_chain")
            V_ = nc.vector

            def moments(k, n, N):
                st = ST[:, 0:n, :]
                m0, m1, v0, v1 = (st[:, :, c] for c in (1, 4, 2, 5))
                V_.tensor_tensor(s1[:, 0:n], m0, m1, ALU.add)
                V_.tensor_tensor(s3[:, 0:n], v0, v1, ALU.add)
                link(V_.tensor_tensor(s2[:, 0:n], m0, m1, ALU.subtract))
                V_.tensor_scalar(mean[:, 0:n], s1[:, 0:n], 0.5, None, ALU.mult)
                V_.tensor_scalar(s3[:, 0:n], s3[:, 0:n], 1.0 / N, EPS, ALU.mult, ALU.add)
                link(V_.scalar_tensor_tensor(out=lnv[:, 0:n], in0=s2[:, 0:n], scalar=0.25, in1=s2[:, 0:n], op0=ALU.mult, op1=ALU.mult))
                V_.tensor_tensor(var[:, 0:n], s3[:, 0:n], lnv[:, 0:n], ALU.add).then_inc(s["ln_var"], 1)
                dve.wait_ge(s["ln_y"], k + 1)
                link(V_.tensor_tensor(s1[:, 0:n], yv[:, 0:n], yv[:, 0:n], ALU.mult))
                link(V_.tensor_tensor(s1[:, 0:n], s1[:, 0:n], var[:, 0:n], ALU.mult))
                link(V_.tensor_scalar(s1[:, 0:n], s1[:, 0:n], -0.5, 1.5, ALU.mult, ALU.add))
                link(V_.tensor_tensor(rstd[:, 0:n], s1[:, 0:n], yv[:, 0:n], ALU.mult))

            def normed(dst, b):
                return V_.tensor_scalar(dst, at(X, b), mean[:, cols(b, 1)], rstd[:, cols(b, 1)], ALU.subtract, ALU.mult)

            dve.wait_ge(s["consts"], 1)
            link(V_.tensor_scalar(pidx[:, 1:2], pidx[:, 0:1], 16, None, ALU.bitwise_and))
            V_.tensor_scalar(par[:, 0:1], pidx[:, 1:2], 0.0, None, ALU.is_equal)
            link(V_.tensor_scalar(par[:, 1:2], pidx[:, 1:2], 0.0, None, ALU.is_gt))

            for q in range(XQ):
                dve.wait_ge(s[f"x_in{q}"], 16)
                for b in range(4 * q, 4 * q + 4):
                    last = V_.bn_stats(ST[:, b, :], X[:, b, :])
            link(last)
            moments(0, NB, D)
            dve.wait_ge(s["small_in"], 16 * 4)
            V_.tensor_tensor(wgate_g[:, 2:4, :], wgate_g[:, 2:4, :], wgate_g[:, 4:6, :], ALU.add).then_inc(s["gw_ready"], 1)
            dve.wait_ge(s["c_in"], 16 * XQ)
            dve.wait_ge(s["wbig_in"], 16 * 3)

            def norm1(b, u, h):
                free_after(dve, s["tr_done"], b)
                V_.tensor_copy(Cu[:, u, :], at(CX, b))
                normed(T[:, u, :], b).then_inc(s["xln_ready"], 1)

            def w_block(b, u, h):
                w, am_, sc_, in_ = W_b(b), S_b(wam, b), S_b(wsc, b), S_b(winv, b)
                V_.tensor_reduce(am_, w, AX.X, ALU.max, apply_absolute_value=True).then_inc(s["w_step"], 1)
                dve.wait_ge(s["w_step"], 5 * b + 1)
                V_.tensor_scalar(sc_, am_, 1.0 / 7.0, TINY, ALU.mult, ALU.max).then_inc(s["w_step"], 1)
                dve.wait_ge(s["w_step"], 5 * b + 2)
                V_.reciprocal(in_, sc_).then_inc(s["w_step"], 1)
                dve.wait_ge(s["w_step"], 5 * b + 3)
                V_.tensor_tensor(w, w, in_.unsqueeze(2).broadcast_to([P, WB, BLK]), ALU.mult).then_inc(s["w_step"], 1)
                dve.wait_ge(s["w_step"], 5 * b + 4)
                V_.tensor_scalar(w, w, ROUND, -ROUND, ALU.add, ALU.add).then_inc(s["w_step"], 1)
            steps(dve, NB, [(norm1, 0), (w_block, 0)])
            dve.wait_ge(s["g_done"], NB)
            V_.tensor_tensor(GA[:, :, :], ps[6][:, 0:NB * 2 * NH0].rearrange("p (b g) -> p b g", b=NB), gb[:, :].unsqueeze(1).broadcast_to([P, NB, 2 * NH0]),
                             ALU.add).then_inc(s["ga_ready"], 1)
            dve.wait_ge(s["ga_ready"], 1)

            fg, ig = GA[:, :, NH0:], GA[:, :, 0:NH0]
            V_.scalar_tensor_tensor(out=az[:, :, :], in0=fg, scalar=-1.0, in1=fg, op0=ALU.mult, op1=ALU.max).then_inc(s["fgate_dve"], 1)
            link(V_.tensor_scalar(lf[:, :, :], fg, 0.0, None, ALU.min))
            dve.wait_ge(s["fgate_act"], 1)
            V_.tensor_tensor(lf[:, :, :], lf[:, :, :], ez[:, :, :], ALU.subtract).then_inc(s["fgate_dve"], 1)
            dve.wait_ge(s["fgate_pe"], 1)
            cs = ps[7][:, 256:256 + NB * NH0].rearrange("p (b h) -> p b h", h=NH0)
            V_.tensor_tensor(AG[:, :, NH0:], ig, cs, ALU.subtract)
            V_.tensor_tensor(Acol[:, :, :], ig, cs, ALU.subtract).then_inc(s["fgate_dve"], 1)
            dve.wait_ge(s["fgate_pe"], 2)
            link(V_.tensor_copy(aT[:, :], ps[7][0:NB * NH0, 0:P]))
            V_.tensor_tensor_scan(mT[:, :], zT[:, :], aT[:, :], -3e38, ALU.add, ALU.max).then_inc(s["fgate_dve"], 1)
            dve.wait_ge(s["fgate_pe"], 3)
            mcol = ps[7][:, P:P + NB * NH0].rearrange("p (b h) -> p b h", h=NH0)
            link(V_.tensor_copy(AG[:, :, 0:NH0], mcol))
            V_.tensor_tensor(nmx[:, :, :], cs, AG[:, :, 0:NH0], ALU.add).then_inc(s["fgate_dve"], 1)

            def norm2(b, u, h):
                free_after(dve, s["tr2_done"], b)
                free_after(dve, s["decay"], b)
                free_after(dve, s["mb_done"], b)
                V_.tensor_copy(MAu[:, u, :], at(AG, b))
                V_.tensor_copy(Cu[:, u, :], at(CX, b))
                normed(T[:, u, :], b).then_inc(s["xln2_ready"], 1)

            def copy_c(b, u, h):
                dve.wait_ge(s["tr2_done"], b + 1)
                free_after(dve, s["qk_done"], b)
                if isinstance(b, int) and b < 2:
                    dve.wait_ge(s["g_done"], NB)
                V_.tensor_scalar(XCT[:, u, 0:2], ps[u][:, 0:2 * P].rearrange("p (k n) -> p k n", k=2), 0.125, None, ALU.mult)
                V_.tensor_copy(XCT[:, u, 2:4], ps[u][:, 2 * P:4 * P].rearrange("p (k n) -> p k n", k=2)).then_inc(s["c_copied"], 1)

            def weigh(b, u, h):
                dve.wait_ge(s["qk_done"], b + 1)
                dve.wait_ge(s["decay"], b + 1)
                free_after(dve, s["av_done"], b)
                V_.scalar_tensor_tensor(out=HC[:, u].rearrange("p (r k) n -> p r (k n)", r=2), in0=HD[:, u].rearrange("p (r k) n -> p r (k n)", r=2),
                                        scalar=1.0, in1=pB[:, :, 0:2 * P], op0=ALU.min, op1=ALU.mult).then_inc(s["c_ready"], 1)

            def finish(b, u, h):
                dve.wait_ge(s["u_copied"], b + 1)
                d = den[:, u]
                rowsum = at(HU, b)[:, :, DH0]
                V_.scalar_tensor_tensor(out=d[:, 0], in0=rowsum, scalar=-1.0, in1=rowsum, op0=ALU.mult, op1=ALU.max).then_inc(s["fin"], 1)
                dve.wait_ge(s["fin"], 5 * b + 1)
                V_.tensor_tensor(d[:, 1], d[:, 0], at(nm, b), ALU.max).then_inc(s["fin"], 1)
                dve.wait_ge(s["fin"], 5 * b + 2)
                V_.tensor_scalar(d[:, 0], d[:, 1], 1e-6, None, ALU.add).then_inc(s["fin"], 1)
                dve.wait_ge(s["fin"], 5 * b + 3)
                V_.reciprocal(d[:, 1], d[:, 0]).then_inc(s["fin"], 1)
                dve.wait_ge(s["fin"], 5 * b + 4)
                V_.tensor_tensor(H[:, cols(b, NH0), :], at(HU, b)[:, :, 0:DH0], d[:, 1].unsqueeze(2).broadcast_to([P, NH0, DH0]), ALU.mult).then_inc(s["fin"], 1)

            def head_stats(b, u, h):
                dve.wait_ge(s["fin"], 5 * b + 5)
                for n in range(NH0):
                    last = V_.bn_stats(ST[:, cols(b * NH0 + n, 1), :].squeeze(1), H[:, cols(b * NH0 + n, 1), :].squeeze(1))
                last.then_inc(s["hst"], 1)
            dve.wait_ge(s["fgate_act"], 2)
            steps(dve, NB, [(norm2, 0), (copy_c, 0), (weigh, 1), (finish, 3), (head_stats, 4)])
            dve.wait_ge(s["hst"], NB)
            moments(1, NB * NH0, DH0)
            def head_norm(b, u, h):
                for n in range(NH0):
                    r = H[:, cols(b * NH0 + n, 1), :].squeeze(1)
                    last = V_.tensor_scalar(r, r, mean[:, cols(b * NH0 + n, 1)], rstd[:, cols(b * NH0 + n, 1)], ALU.subtract, ALU.mult)
                last.then_inc(s["h_normed"], 1)

            def add_heads(b, u, h):
                dve.wait_ge(s["h_scaled"], b + 1)
                V_.tensor_tensor(at(X, b), at(X, b), H_b(b), ALU.add).then_inc(s["x1_ready"], 1)

            def stats2(b, u, h):
                dve.wait_ge(s["x1_ready"], b + 1)
                V_.bn_stats(at(ST, b), at(X, b)).then_inc(s["row_stats"], 1)
            steps(dve, NB, [(head_norm, 0), (add_heads, 2), (stats2, 3)])
            dve.wait_ge(s["row_stats"], NB)
            moments(2, NB, D)

            def global_max(k, n):
                dve.wait_ge(s["gmT"], k + 1)
                link(V_.tensor_reduce(gr[0:n, 1:2], ps[5 if k == 3 else 0][0:n, 0:P], AX.X, ALU.max))
                V_.tensor_scalar(gd[0:n, 0:n], ident[0:n, 0:n], gr[0:n, 1:2], None, ALU.mult).then_inc(s["gr_ready"], 1)
                dve.wait_ge(s["gm_all"], k + 1)

            def xl(b, u, h):
                normed(at(XL, b), b).then_inc(s["xl_ready"], 1)

            def xl_max(b, u, h):
                dve.wait_ge(s["xl_ready"], b + 1)
                V_.tensor_reduce(am[:, 0, cols(b, 1)], at(XL, b), AX.X, ALU.max, apply_absolute_value=True).then_inc(s["xl_max"], 1)
            steps(dve, NB, [(xl, 0), (xl_max, 1)])
            dve.wait_ge(s["xl_max"], NB)
            V_.tensor_reduce(gm[:, 0:1], am[:, 0, 0:NB], AX.X, ALU.max).then_inc(s["gm_ready"], 1)
            global_max(0, 1)
            link(V_.tensor_scalar(sc[:, 0:1], ps[0][:, 256:257], 1.0 / QMAX, TINY, ALU.mult, ALU.max))
            link(V_.reciprocal(sc[:, 1:2], sc[:, 0:1]))

            def x_int(b, u):
                V_.tensor_scalar(at(XL, b), at(XL, b), sc[:, 1:2], ROUND, ALU.mult, ALU.add).then_inc(s["offset"], 1)
                dve.wait_ge(s["offset"], b + 1)
                free_after(dve, s["tr3_done"], b)
                V_.tensor_scalar(T[:, u, :], at(XL, b), -ROUND, QMAX, ALU.add, ALU.min).then_inc(s["xi_ready"], 1)

            def piece_max(t, name, c, f):
                dve.wait_ge(s[f"{name}_out"], c * FT + f + 1)
                V_.tensor_reduce(am[:, 0 if name == "gate" else 1, cols(c * FT + f, 1)], t[:, f, cols(c, 512)], AX.X, ALU.max,
                                 apply_absolute_value=True).then_inc(s[f"{name}_max"], 1)

            def gate_chunk(c):
                for j in range(4):
                    x_int(4 * c + j, j % 2)
                for f in range(FT):
                    piece_max(G, "gate", c, f)
            gate_chunk(0)
            with dve.Fori(1, 4) as c:
                gate_chunk(c)
            dve.wait_ge(s["gate_max"], 4 * FT)
            V_.tensor_reduce(gm[:, 0:1], am[:, 0, :], AX.X, ALU.max).then_inc(s["gm_ready"], 1)
            global_max(1, 1)
            link(V_.tensor_scalar(sc[:, 3:4], ps[0][:, 256:257], sc[:, 0:1], None, ALU.mult))
            link(V_.tensor_scalar(sc[:, 5:6], sc[:, 3:4], 1.0 / QMAX, TINY, ALU.mult, ALU.max))
            link(V_.reciprocal(sc[:, 9:10], sc[:, 5:6]))
            link(V_.tensor_scalar(sc[:, 7:8], sc[:, 9:10], sc[:, 0:1], None, ALU.mult))
            V_.tensor_scalar(sc[:, 14:15], sc[:, 5:6], 1.0 / 65536.0, None, ALU.mult).then_inc(s["sc_gate"], 1)

            def g_to_int(b):
                V_.tensor_scalar(F_b(G, b), F_b(G, b), sc[:, 7:8], ROUND, ALU.mult, ALU.add).then_inc(s["offset"], 1)
                dve.wait_ge(s["offset"], NB + b + 1)
                V_.tensor_scalar(F_b(G, b), F_b(G, b), -ROUND, QMAX, ALU.add, ALU.min).then_inc(s["g_int"], 1)

            def sig_to_int(b, u):
                dve.wait_ge(s["sig_b"], b + 1)
                V_.tensor_scalar(SG[:, u], SG[:, u], -ROUND, 65535.0, ALU.add, ALU.min).then_inc(s["sg_int"], 1)

            def gs_max(b):
                dve.wait_ge(s["gs_done"], b + 1)
                V_.tensor_reduce(am[:, 0, cols(b, 1)], F_b(G, b), AX.XY, ALU.max, apply_absolute_value=True).then_inc(s["gs_max"], 1)

            def up_chunk(c):
                last = isinstance(c, int) and c == 3
                for j in range(4):
                    if not (last and j >= 3):
                        g_to_int(4 * c + j + 1)
                    sig_to_int(4 * c + j, j % 2)
                    if not (isinstance(c, int) and c == 0 and j < 1):
                        gs_max(4 * c + j - 1)
                    piece_max(U, "up", c, j)
                piece_max(U, "up", c, 4)
                piece_max(U, "up", c, 5)
            g_to_int(0)
            up_chunk(0)
            with dve.Fori(1, 3) as c:
                up_chunk(c)
            up_chunk(3)
            gs_max(NB - 1)
            dve.wait_ge(s["gs_max"], NB)
            V_.tensor_reduce(gm[:, 0:1], am[:, 0, 0:NB], AX.X, ALU.max)
            V_.tensor_reduce(gm[:, 1:2], am[:, 1, :], AX.X, ALU.max).then_inc(s["gm_ready"], 1)
            global_max(2, 2)
            gs_all, up_all = ps[0][:, 256:257], ps[0][:, 257:258]
            link(V_.tensor_scalar(sc[:, 15:16], gs_all, sc[:, 14:15], 1.0 / QMAX, ALU.mult, ALU.mult))
            link(V_.tensor_scalar(sc[:, 2:3], up_all, sc[:, 0:1], 1.0 / QMAX, ALU.mult, ALU.mult))
            link(V_.tensor_scalar(sc[:, 15:16], sc[:, 15:16], TINY, None, ALU.max))
            link(V_.tensor_scalar(sc[:, 4:5], sc[:, 2:3], TINY, None, ALU.max))
            link(V_.reciprocal(sc[:, 16:17], sc[:, 15:16]))
            link(V_.reciprocal(sc[:, 8:9], sc[:, 4:5]))
            link(V_.tensor_scalar(sc[:, 10:11], sc[:, 16:17], sc[:, 14:15], None, ALU.mult))
            V_.tensor_scalar(sc[:, 6:7], sc[:, 8:9], sc[:, 0:1], None, ALU.mult).then_inc(s["sc_up"], 1)

            def g2_int(b, u, h):
                V_.tensor_scalar(F_b(G, b), F_b(G, b), sc[:, 10:11], ROUND, ALU.mult, ALU.add).then_inc(s["g2"], 1)
                dve.wait_ge(s["g2"], 2 * b + 1)
                V_.tensor_scalar(F_b(G, b), F_b(G, b), -ROUND, QMAX, ALU.add, ALU.min).then_inc(s["g2"], 1)
                dve.wait_ge(s["g2"], 2 * b + 2)

            def product(b, u, h):
                dve.wait_ge(s["u_b"], b + 1)
                V_.scalar_tensor_tensor(out=F_b(U, b), in0=F_b(U, b), scalar=-ROUND, in1=F_b(G, b), op0=ALU.add, op1=ALU.mult).then_inc(s["prod"], 1)
                dve.wait_ge(s["prod"], b + 1)
                V_.tensor_reduce(am[:, 0, cols(b, 1)], F_b(U, b), AX.XY, ALU.max, apply_absolute_value=True).then_inc(s["prod_max"], 1)
            steps(dve, NB, [(g2_int, 0), (product, 0)])
            dve.wait_ge(s["prod_max"], NB)
            V_.tensor_reduce(gm[:, 0:1], am[:, 0, 0:NB], AX.X, ALU.max).then_inc(s["gm_ready"], 1)
            global_max(3, 1)
            link(V_.tensor_scalar(sc[:, 17:18], sc[:, 15:16], sc[:, 4:5], None, ALU.mult))
            link(V_.tensor_scalar(sc[:, 18:19], ps[5][:, 256:257], sc[:, 17:18], 1.0 / QMAX, ALU.mult, ALU.mult))
            link(V_.tensor_scalar(sc[:, 18:19], sc[:, 18:19], TINY, None, ALU.max))
            link(V_.reciprocal(sc[:, 19:20], sc[:, 18:19]))
            link(V_.tensor_scalar(sc[:, 13:14], sc[:, 19:20], sc[:, 17:18], None, ALU.mult))

            def o_int(b, u, h):
                V_.tensor_scalar(F_b(U, b), F_b(U, b), sc[:, 13:14], ROUND, ALU.mult, ALU.add).then_inc(s["offset"], 1)
                dve.wait_ge(s["offset"], 2 * NB + b + 1)
                free_after(dve, s["down_done"], b)
                V_.tensor_scalar(OT[:, u], F_b(U, b), -ROUND, QMAX, ALU.add, ALU.min).then_inc(s["oi_ready"], 1)

            def residual(b, u, h):
                dve.wait_ge(s["down_done"], b + 1)
                V_.scalar_tensor_tensor(out=at(X, b), in0=ps[6 + u][:, 0:D], scalar=sc[:, 18:19], in1=at(X, b), op0=ALU.mult, op1=ALU.add).then_inc(s["x2_ready"], 1)

            def stats3(b, u, h):
                dve.wait_ge(s["x2_ready"], b + 1)
                V_.bn_stats(at(ST, b), at(X, b)).then_inc(s["row_stats"], 1)
            steps(dve, NB, [(o_int, 0), (residual, 1), (stats3, 2)])
            dve.wait_ge(s["row_stats"], 2 * NB)
            V_.tensor_scalar(bq[:, :], bq[:, :], 0.25, None, ALU.mult)
            moments(3, NB, D)

            def add_attn(b, u, h):
                dve.wait_ge(s["o_done"], b + 1)
                dve.wait_ge(s["bo_added"], b + 1)
                V_.tensor_tensor(at(X, b), ps[4][:, 2 * P:4 * P], at(X, b), ALU.add).then_inc(s["x3_ready"], 1)

            def stats4(b, u, h):
                dve.wait_ge(s["x3_ready"], b + 1)
                V_.bn_stats(at(ST, b), at(X, b)).then_inc(s["row_stats"], 1)

            def norm3(b, u, h):
                free_after(dve, s["c_tr"], b)
                normed(T[:, u, :], b).then_inc(s["xn3"], 1)

            def attn_out(b, u, h):
                dve.wait_ge(s["pv_done"], b + 1)
                o = ps[5][:, 0:NH1 * (DH1 + 1)].rearrange("p (h d) -> p h d", h=NH1)
                V_.reciprocal(rs[:, u, :], o[:, :, DH1]).then_inc(s["rs_ready"], 1)
                dve.wait_ge(s["rs_ready"], b + 1)
                free_after(dve, s["a_tr"], b)
                V_.tensor_tensor(AO[:, u, :].rearrange("p (h d) -> p h d", h=NH1), o[:, :, 0:DH1],
                                 rs[:, u, :].unsqueeze(2).broadcast_to([P, NH1, DH1]), ALU.mult).then_inc(s["ao_ready"], 1)

            def softmax(b, u, h):
                dve.wait_ge(s["scores"], b + 1)
                sco = pA[:, :, :].rearrange("p j (k n) -> p (j k) n", n=P)
                V_.tensor_reduce(rm[:, u, :], sco, AX.X, ALU.max).then_inc(s["rm_ready"], 1)
                dve.wait_ge(s["rm_ready"], b + 1)
                free_after(dve, s["pv_done"], b)
                V_.tensor_tensor(PR[:, u], sco, rm[:, u, :].unsqueeze(2).broadcast_to([P, NH1, P]), ALU.subtract).then_inc(s["s_sub"], 1)
            steps(dve, NB, [(softmax, 2), (add_attn, 4), (attn_out, 3), (norm3, 0), (stats4, 4)])
            dve.wait_ge(s["row_stats"], 3 * NB)
            moments(4, NB, D)

            def norm4(b, u, h):
                free_after(dve, s["d_tr"], b)
                normed(T[:, u, :], b).then_inc(s["xn4"], 1)
                normed(at(XR, b)[:, 0:D], b).then_inc(s["xr_ready"], 1)
            steps(dve, NB, [(norm4, 0)])
            dve.wait_ge(s["tables"], 1)
            V_.tensor_copy(cidx[:, :], cidx_f)
            V_.tensor_copy(ids[:, :, :], ids_f)
            dve.wait_ge(s["d_lg"], NB)
            logits = ps[2][:, 0:NB * NE].rearrange("p (b e) -> p b e", b=NB)

            def per_e(ap):
                return ap.unsqueeze(2).broadcast_to([P, NB, NE])
            link(V_.tensor_reduce(r1[:, :], logits, AX.X, ALU.max))
            V_.tensor_tensor(LG[:, :, :], logits, per_e(r1[:, :]), ALU.subtract).then_inc(s["lg_sub"], 1)
            dve.wait_ge(s["lg_exp"], 1)
            link(V_.tensor_reduce(r1[:, :], LG[:, :, :], AX.X, ALU.add))
            link(V_.reciprocal(r1[:, :], r1[:, :]))
            V_.tensor_tensor(LW[:, :, :], LG[:, :, :], per_e(r1[:, :]), ALU.mult)
            V_.tensor_tensor(LG[:, :, :], LG[:, :, :], per_e(r1[:, :]), ALU.mult).then_inc(s["probs"], 1)
            dve.wait_ge(s["probs"], 1)
            for k in range(TOPK):
                link(V_.tensor_reduce(gates[:, k, :], LW[:, :, :], AX.X, ALU.max))
                link(V_.tensor_tensor(q1[:, :, :], LW[:, :, :], per_e(gates[:, k, :]), ALU.is_equal))
                link(V_.tensor_tensor(q1[:, :, :], q1[:, :, :], rank8[:, :, :], ALU.mult))
                link(V_.tensor_reduce(r1[:, :], q1[:, :, :], AX.X, ALU.max))
                link(V_.tensor_tensor(OH[:, k], q1[:, :, :], per_e(r1[:, :]), ALU.is_equal))
                if k + 1 < TOPK:
                    link(V_.scalar_tensor_tensor(out=LW[:, :, :], in0=OH[:, k], scalar=-2.0, in1=LW[:, :, :], op0=ALU.mult, op1=ALU.add))
            V_.tensor_copy(OHb[:, :], OH[:, :, :, :].rearrange("p k b e -> p (k b e)")).then_inc(s["oh_ready"], 1)
            dve.wait_ge(s["cnt_done"], 1)
            for g in range(NG):
                for k in range(TOPK):
                    last = V_.tensor_copy(tot[:, g, :, k, :], ps[5][:, 0:TOPK * NB * NE].rearrange("p (k g t e) -> p k g e t", k=TOPK, g=NG, t=TG)[:, k, g])
            link(last)
            link(V_.tensor_tensor_scan(inc[:, :, :, :, :].rearrange("p g e k t -> p (g e k t)"), segm[:, :],
                                       tot[:, :, :, :, :].rearrange("p g e k t -> p (g e k t)"), 0.0, ALU.mult, ALU.add))
            link(V_.tensor_tensor(inc[:, :, :, :, :].rearrange("p g e k t -> p (g e k t)"), inc[:, :, :, :, :].rearrange("p g e k t -> p (g e k t)"),
                                  tot[:, :, :, :, :].rearrange("p g e k t -> p (g e k t)"), ALU.subtract))
            for g in range(NG):
                for k in range(TOPK):
                    last = V_.tensor_tensor(pos[:, k, g * TG:(g + 1) * TG, :],
                                            ps[4][:, 0:TOPK * NB * NE].rearrange("p (k g t e) -> p k g t e", k=TOPK, g=NG, t=TG)[:, k, g],
                                            inc[:, g, :, k, :].rearrange("p e t -> p t e"), ALU.add)
            link(last)
            link(V_.scalar_tensor_tensor(out=tmp[:, :, :, :], in0=pos[:, :, :, :], scalar=1.0, in1=OH[:, :, :, :], op0=ALU.add, op1=ALU.mult))
            link(V_.tensor_tensor(place[:, :, :], tmp[:, 0], tmp[:, 1], ALU.add))
            V_.tensor_scalar(shift[:, :, :], place[:, :, :], CAP + 1.0, 4.0 * SELW, ALU.is_ge, ALU.mult)
            link(V_.tensor_scalar(q1[:, TG:, :], place[:, TG:, :], P + 1.0, float(SPARE), ALU.is_ge, ALU.mult))
            link(V_.tensor_tensor(place[:, :, :], place[:, :, :], shift[:, :, :], ALU.add))
            link(V_.tensor_tensor(place[:, TG:, :], place[:, TG:, :], q1[:, TG:, :], ALU.add))
            link(V_.tensor_copy(placeb[:, :, :], place[:, :, :]))

            def select(e, u, h):
                free_after(dve, s["id_done"], e)
                V_.tensor_tensor(SEL[:, u], placeb[:, :, cols(e, 1)].broadcast_to([P, NB, SELW]),
                                 cidx[:, :].unsqueeze(1).broadcast_to([P, NB, SELW]), ALU.is_equal).then_inc(s["sel_ready"], 1)

            def number(e, u, h):
                dve.wait_ge(s["id_done"], e + 1)
                chunks = ((P, 0, 2), (ROWS - 2 * P, 2, 3))
                for n, c, c1 in chunks:
                    last = V_.tensor_reduce(num[0:n, u, c:c1], ps[7][0:n, 2 * c:2 * c1].rearrange("p (c i) -> p c i", i=2), AX.X, ALU.add)
                last.then_inc(s["num_ready"], 1)
                dve.wait_ge(s["num_ready"], e + 1)
                for n, c, c1 in chunks:
                    last = V_.tensor_scalar(token[0:n, cols(e, 1), c:c1].squeeze(1), num[0:n, u, c:c1], float(NB * S), None, ALU.add)
                last.then_inc(s["token_ready"], 1)

            def gate_column(e, u, h):
                dve.wait_ge(s[f"xe_in{u}"], 48 * (h + 1))
                free_after(dve, s["y_ready"], e, 3)
                V_.tensor_copy(gcol[:, u, :], XE[:, u, :, bass.ds(D + e, 1)].squeeze(2)).then_inc(s["gcol_ready"], 1)

            def add_rows(e, u, h):
                dve.wait_ge(s["yg_in"], 48 * (e + 1))
                dve.wait_ge(s["gcol_ready"], e + 1)
                for c in range(3):
                    n = P if c < 2 else ROWS - 2 * P
                    dve.wait_ge(s["ec_done"], e * 3 + c + 1)
                    V_.scalar_tensor_tensor(out=YG[0:n, c, :], in0=ps[4 + c][0:n, 0:D], scalar=gcol[0:n, u, c:c + 1], in1=YG[0:n, c, :],
                                            op0=ALU.mult, op1=ALU.add).then_inc(s["y_ready"], 1)
            steps(dve, NE, [(number, 1), (select, 0), (add_rows, 4), (gate_column, 2)])

        @block.tensor
        def _(pe):
            mm, tr = nc.tensor.matmul, nc.tensor.transpose
            pe.wait_ge(s["consts"], 1)
            def ctx_cols(u, k):
                return Cu[:, u, k * P:(k + 1) * P]

            def turn(b, u, h):
                pe.wait_ge(s["xln_ready"], b + 1)
                free_after(pe, s["xct_ready"], b)
                for k in range(KD):
                    tr(ps[u][:, k * P:(k + 1) * P], T[:, u, k * P:(k + 1) * P], ident[:, :])
                for k in range(KD):
                    last = tr(ps[u][:, (2 + k) * P:(3 + k) * P], ctx_cols(u, k), ident[:, :])
                last.then_inc(s["tr_done"], 1)

            def gates(b, u, h):
                pe.wait_ge(s["xct_ready"], b + 1)
                for k in range(4):
                    last = mm(ps[6][:, cols(b, 2 * NH0)], XCT[:, u, k, :], wgate_g[:, k, :], start=(k == 0), stop=(k == 3))
                last.then_inc(s["g_done"], 1)
            pe.wait_ge(s["gw_ready"], 1)
            steps(pe, NB, [(turn, 0), (gates, 1)])

            pe.wait_ge(s["fgate_dve"], 2)
            mm(ps[7][:, 256:256 + NB * NH0], tri[:, :], lf[:, :, :].rearrange("p b h -> p (b h)"), start=True, stop=True).then_inc(s["fgate_pe"], 1)
            pe.wait_ge(s["fgate_dve"], 3)
            tr(ps[7][0:NB * NH0, 0:P], Acol[:, :, :].rearrange("p b h -> p (b h)"), ident[:, :]).then_inc(s["fgate_pe"], 1)
            pe.wait_ge(s["fgate_dve"], 4)
            tr(ps[7][:, P:P + NB * NH0], mT[:, :], ident[0:NB * NH0, 0:NB * NH0]).then_inc(s["fgate_pe"], 1)

            def turn2(b, u, h):
                pe.wait_ge(s["xln2_ready"], b + 1)
                free_after(pe, s["c_copied"], b)
                for k in range(KD):
                    tr(ps[u][:, k * P:(k + 1) * P], T[:, u, k * P:(k + 1) * P], ident[:, :])
                for k in range(KD):
                    last = tr(ps[u][:, (2 + k) * P:(3 + k) * P], ctx_cols(u, k), ident[:, :])
                last.then_inc(s["tr2_done"], 1)

            def spread_max(b, u, h):
                free_after(pe, s["decay"], b)
                for n in range(NH0):
                    last = tr(ps[2 + u][:, n * P:(n + 1) * P], MAu[:, u, n:n + 1].broadcast_to([P, P]), ident[:, :])
                last.then_inc(s["mb_done"], 1)

            def scores0(b, u, h):
                pe.wait_ge(s["c_copied"], b + 1)
                if not (isinstance(b, int) and b < 1):
                    pe.wait_ge(s["c_ready"], b)
                for n in range(NH0):
                    r = DH0 * (n % 2)
                    last = mm(pB[:, n % 2, (n // 2) * P:(n // 2 + 1) * P], XCT[r:r + DH0, u, 2 + n // 2, :], XCT[r:r + DH0, u, n // 2, :], start=True, stop=True)
                last.then_inc(s["qk_done"], 1)

            def values0(b, u, h):
                pe.wait_ge(s["c_masked"], b + 1)
                pe.wait_ge(s["v_copied"], b + 1)
                free_after(pe, s["u_copied"], b)
                if isinstance(b, int) and b == 0:
                    pe.wait_ge(s["fgate_dve"], 5)
                w = DH0 + 1
                for n in range(NH0):
                    last = mm(pC[:, u, n * w:(n + 1) * w], HC[:, u, 2 * (n % 2) + n // 2, :], VU[:, u, n, :], start=True, stop=True)
                last.then_inc(s["av_done"], 1)
            steps(pe, NB, [(turn2, 0), (spread_max, 0), (scores0, 1), (values0, 2)])

            pe.wait_ge(s["decay"], NB)
            pe.wait_ge(s["w_q"], NB)
            for n in range(13):
                if n >= 2:
                    pe.wait_ge(s["wtr_copied"], n - 1)
                if n >= 9:
                    pe.wait_ge(s[f"w{'qkvo'[n - 9]}_in"], 16)
                for k in range(2):
                    for c in range(2):
                        if n < 6:
                            src = WN[:, n // 3, (2 * (n % 3) + c) * D + k * P:(2 * (n % 3) + c) * D + (k + 1) * P]
                        elif n < 9:
                            src = WN[:, 2, c * FF + (2 * (n - 6) + k) * P:c * FF + (2 * (n - 6) + k + 1) * P]
                        else:
                            src = LN[:, n - 9, c, k * P:(k + 1) * P]
                        last = tr(ps[2 + n % 2][:, (2 * k + c) * P:(2 * k + c + 1) * P], src, ident[:, :])
                last.then_inc(s["wtr_done"], 1)

            def whole_max(k, n):
                pe.wait_ge(s["gm_ready"], k + 1)
                bank = ps[5 if k == 3 else 0]
                tr(bank[0:n, 0:P], gm[:, 0:n], ident[:, :]).then_inc(s["gmT"], 1)
                pe.wait_ge(s["gr_ready"], k + 1)
                mm(bank[:, 256:256 + n], ones[0:n, :], gd[0:n, 0:n], start=True, stop=True).then_inc(s["gm_all"], 1)

            pe.wait_ge(s["wtr_copied"], 13)
            pe.wait_ge(s["u_copied"], NB)
            whole_max(0, 1)

            def turn3(b, u):
                pe.wait_ge(s["xi_ready"], b + 1)
                free_after(pe, s["xit_ready"], b)
                for k in range(KD):
                    last = tr(ps[u][:, k * P:(k + 1) * P], T[:, u, k * P:(k + 1) * P], ident[:, :])
                last.then_inc(s["tr3_done"], 1)

            def product(w, name, c, f):
                for k in range(KD):
                    last = mm(ps[2 + f][:, :], w[:, k, f * P:(f + 1) * P], XITv[:, k, cols(c, 512)], start=(k == 0), stop=(k == KD - 1))
                last.then_inc(s[f"{name}_done"], 1)

            def gate_chunk(c):
                for j in range(4):
                    turn3(4 * c + j, j % 2)
                pe.wait_ge(s["xit_ready"], 4 * c + 4)
                for f in range(FT):
                    if not isinstance(c, int):
                        pe.wait_ge(s["gate_out"], (c - 1) * FT + f + 1)
                    product(wgtT, "gate", c, f)
            gate_chunk(0)
            with pe.Fori(1, 4) as c:
                gate_chunk(c)

            def up_chunk(c):
                for f in range(FT):
                    if isinstance(c, int):
                        pe.wait_ge(s["gate_out"], 3 * FT + f + 1)
                    else:
                        pe.wait_ge(s["up_out"], (c - 1) * FT + f + 1)
                    product(wupT, "up", c, f)
            whole_max(1, 1)
            up_chunk(0)
            with pe.Fori(1, 4) as c:
                up_chunk(c)
            whole_max(2, 2)

            def turn4(b, u, h):
                pe.wait_ge(s[f"ctx_in{u}"], (h + 1) * 16)
                if isinstance(b, int) and b == 0:
                    pe.wait_ge(s["sc_up"], 1)
                free_after(pe, s["xct4_ready"], b)
                for k in range(KD):
                    last = tr(ps[u][:, k * P:(k + 1) * P], ctx_cols(u, k), ident[:, :])
                last.then_inc(s["tr4_done"], 1)

            def project(b, u, h):
                pe.wait_ge(s["xct4_ready"], b + 1)
                free_after(pe, s["kv_copied"], b)
                for e in range(KD):
                    for k in range(KD):
                        mm(ps[2 + u][:, e * P:(e + 1) * P], wT[1][:, k, e * P:(e + 1) * P], XCT[:, u, 2 + k, :], start=(k == 0), stop=(k == KD - 1))
                for k in range(KD):
                    last = mm(ps[2 + u][:, 2 * P:4 * P], XCT[:, u, 2 + k, :], wT[2][:, k, :], start=(k == 0), stop=(k == KD - 1))
                last.then_inc(s["kv_done"], 1)
            pe.wait_ge(s["up_out"], 4 * FT)
            steps(pe, NB, [(turn4, 0), (project, 1)])
            whole_max(3, 1)

            def down(b, u, h):
                pe.wait_ge(s["oi_ready"], b + 1)
                free_after(pe, s["x2_ready"], b)
                for f in range(FT):
                    last = mm(ps[6 + u][:, 0:D], OT[:, u, f, :], wdnT[:, f, :], start=(f == 0), stop=(f == FT - 1))
                last.then_inc(s["down_done"], 1)
            steps(pe, NB, [(down, 0)])

            def c_turn(b, u, h):
                pe.wait_ge(s["xn3"], b + 1)
                if isinstance(b, int) and b < 4:
                    if b >= 1:
                        pe.wait_ge(s["qt_ready"], b)
                else:
                    pe.wait_ge(s["x3_ready"], b - 3)
                for k in range(KD):
                    last = tr(ps[4][:, k * P:(k + 1) * P], T[:, u, k * P:(k + 1) * P], ident[:, :])
                last.then_inc(s["c_tr"], 1)

            def c_query(b, u, h):
                pe.wait_ge(s["c_xt"], b + 1)
                for e in range(KD):
                    for k in range(KD):
                        last = mm(ps[4][:, (2 + e) * P:(3 + e) * P], wT[0][:, k, e * P:(e + 1) * P], XCT[:, u, k, :], start=(k == 0), stop=(k == KD - 1))
                last.then_inc(s["c_q"], 1)

            def c_scores(b, u, e):
                for j in range(4):
                    last = mm(ps[j][:, 2 * e * P:(2 * e + 2) * P], QT[32 * j:32 * j + 32, u, e, :],
                              KM[32 * j:32 * j + 32, u, e, :, :].rearrange("p r n -> p (r n)"), start=True, stop=True)
                return last

            def scores_first(b, u, h):
                pe.wait_ge(s["qt_ready"], b + 1)
                pe.wait_ge(s["km_ready"], b + 1)
                if not (isinstance(b, int) and b < 1):
                    pe.wait_ge(s["s_sub"], b)
                c_scores(b, u, 0)

            def scores_rest(b, u, h):
                c_scores(b, u, 1).then_inc(s["scores"], 1)

            def turn_group(b, u, g):
                if not (isinstance(b, int) and 4 * b + g < 2):
                    pe.wait_ge(s["pt_ready"], 4 * b + g - 1)
                for n in range(4):
                    last = tr(pC[:, g % 2, n * P:(n + 1) * P], PR[:, u, 4 * g + n, :], ident[:, :])
                last.then_inc(s["pt_tr"], 1)

            def value_group(b, u, g):
                w = DH1 + 1
                pe.wait_ge(s["pt_ready"], 4 * b + g + 1)
                for n in range(4):
                    head = 8 * (n // 2) + 2 * g + n % 2
                    last = mm(ps[5][:, head * w:(head + 1) * w], PT[:, u, 4 * g + n, :], at(V, b)[:, head, :], start=True, stop=True)
                return last

            def values_first(b, u, h):
                pe.wait_ge(s["p_ready"], b + 1)
                turn_group(b, u, 0)
                turn_group(b, u, 1)
                if not (isinstance(b, int) and b < 1):
                    pe.wait_ge(s["ao_ready"], b)
                value_group(b, u, 0)

            def values_rest(b, u, h):
                turn_group(b, u, 2)
                value_group(b, u, 1)
                turn_group(b, u, 3)
                value_group(b, u, 2)
                value_group(b, u, 3).then_inc(s["pv_done"], 1)

            def a_turn(b, u, h):
                pe.wait_ge(s["ao_ready"], b + 1)
                if isinstance(b, int) and b + 3 >= NB:
                    pe.wait_ge(s["x3_ready"], b)
                else:
                    pe.wait_ge(s["qt_ready"], b + 4)
                for k in range(KD):
                    last = tr(ps[4][:, k * P:(k + 1) * P], AO[:, u, k * P:(k + 1) * P], ident[:, :])
                last.then_inc(s["a_tr"], 1)

            def a_out(b, u, h):
                pe.wait_ge(s["at_ready"], b + 1)
                for k in range(KD):
                    last = mm(ps[4][:, 2 * P:4 * P], AT[:, u, k, :], wT[3][:, k, :], start=(k == 0), stop=(k == KD - 1))
                last.then_inc(s["o_done"], 1)
            steps(pe, NB, [(scores_first, 1), (c_turn, 0), (scores_rest, 1), (c_query, 0), (values_first, 2), (a_turn, 3), (values_rest, 2), (a_out, 3)])

            def d_turn(b, u, h):
                pe.wait_ge(s["xn4"], b + 1)
                free_after(pe, s["d_xt"], b)
                for k in range(KD):
                    last = tr(ps[u][:, k * P:(k + 1) * P], T[:, u, k * P:(k + 1) * P], ident[:, :])
                last.then_inc(s["d_tr"], 1)

            def d_logits(b, u, h):
                pe.wait_ge(s["d_xt"], b + 1)
                for k in range(KD):
                    last = mm(ps[2][:, cols(b, NE)], XCT[:, u, k, :], wrt[:, k, :], start=(k == 0), stop=(k == KD - 1))
                last.then_inc(s["d_lg"], 1)
            steps(pe, NB, [(d_turn, 0), (d_logits, 1)])
            pe.wait_ge(s["oh_ready"], 1)
            mm(ps[4][:, 0:TOPK * NB * NE], stri[:, :], OHb[:, :], start=True, stop=True)
            mm(ps[5][:, 0:TOPK * NB * NE], onesb[:, :], OHb[:, :], start=True, stop=True).then_inc(s["cnt_done"], 1)

            def e_tokens(e, u, h):
                pe.wait_ge(s["sel_ready"], e + 1)
                if not (isinstance(e, int) and e < 1):
                    pe.wait_ge(s["token_ready"], e)
                for c, tiles in ((0, range(TG)), (1, range(TG, NB)), (2, range(NB))):
                    n = P if c < 2 else ROWS - 2 * P
                    for b in tiles:
                        last = mm(ps[7][0:n, 2 * c:2 * c + 2], SEL[:, u, b, 0:P] if c < 2 else SEL[:, u, b, P:], ids[:, b, :],
                                  start=(b == tiles[0]), stop=(b == tiles[-1]))
                last.then_inc(s["id_done"], 1)

            def e_turn(e, u, h):
                pe.wait_ge(s[f"xe_in{u}"], (h + 1) * 48)
                if not (isinstance(e, int) and e < 1):
                    pe.wait_ge(s["xet_ready"], e)
                for k in range(KD):
                    for c in range(3):
                        n = P if c < 2 else ROWS - 2 * P
                        last = tr(ps[k][:, c * P:c * P + n], XE[0:n, u, c, k * P:(k + 1) * P], ident[0:n, 0:n])
                last.then_inc(s["xe_tr"], 1)

            def e_hidden(e, u, h):
                pe.wait_ge(s["xet_ready"], e + 1)
                pe.wait_ge(s[f"wi_in{u}"], (h + 1) * 16)
                for f in range(NFT):
                    if not (isinstance(e, int) and e * NFT + f < 2):
                        pe.wait_ge(s["h_relu"], e * NFT + f - 1)
                    for k in range(KD):
                        last = mm(ps[2 + f % 2][:, 0:ROWS], WI[:, u, k, f * P:(f + 1) * P], XET[:, u, k, :], start=(k == 0), stop=(k == KD - 1))
                    last.then_inc(s["h_done"], 1)

            def e_out(e, u, h):
                pe.wait_ge(s["h_relu"], (e + 1) * NFT)
                pe.wait_ge(s[f"wo_in{u}"], (h + 1) * 16)
                if not (isinstance(e, int) and e < 1):
                    pe.wait_ge(s["y_ready"], 3 * e)
                for c in range(3):
                    n = P if c < 2 else ROWS - 2 * P
                    for f in range(NFT):
                        last = mm(ps[4 + c][0:n, 0:D], HT[:, u, f, c * P:c * P + n], WO[:, u, f, :], start=(f == 0), stop=(f == NFT - 1))
                    last.then_inc(s["ec_done"], 1)
            steps(pe, NE, [(e_tokens, 0), (e_hidden, 3), (e_turn, 2), (e_out, 4)])


_INS = ["x", "ctx_1024", "L0_xattn_igate_kernel", "L0_xattn_igate_bias", "L0_xattn_fgate_kernel", "L0_xattn_fgate_bias",
        "L0_xattn_outnorm_scale", "L0_ffn_w_gate", "L0_ffn_w_up", "L0_ffn_w_down", "L1_xattn_w_q", "L1_xattn_b_q",
        "L1_xattn_w_k", "L1_xattn_b_k", "L1_xattn_w_v", "L1_xattn_b_v", "L1_xattn_w_o", "L1_xattn_b_o",
        "L1_ffn_w_router", "L1_ffn_wi", "L1_ffn_wo"]


def kernel(**inputs):
    import numpy as _np
    import concourse.bacc as _bacc
    from concourse import mybir as _mybir
    from concourse.bass_utils import run_bass_kernel_spmd as _run

    nc = _bacc.Bacc("TRN2", target_bir_lowering=False, num_devices=1)
    arrays, args = {}, {}
    for name in _INS:
        a = _np.ascontiguousarray(inputs[name])
        arrays[f"in_{name}"] = a
        args[name] = nc.dram_tensor(f"in_{name}", a.shape, _mybir.dt.from_np(a.dtype), kind="ExternalInput").ap()
    shape = tuple(arrays["in_x"].shape)
    out = nc.dram_tensor("out_0", shape, _mybir.dt.float32, kind="ExternalOutput").ap()
    build(nc, args, out)
    r = _run(nc, [arrays], core_ids=[0])
    return r.results[0]["out_0"]
```

```python
from contextlib import ExitStack

import numpy as np
import concourse.bass as bass
from concourse import mybir

F32 = mybir.dt.float32
BF16 = mybir.dt.bfloat16
I32 = mybir.dt.int32
U32 = mybir.dt.uint32
I16 = mybir.dt.int16
U16 = mybir.dt.uint16
ALU = mybir.AluOpType
ACT = mybir.ActivationFunctionType
AX = mybir.AxisListType

P = 128
ROUND = 12582912.0
QMAX = 32767.0
TINY = 1e-12
WIDE = 64
EPS = 1e-5


def steps(eng, n, stages):
    deepest = max(lag for _, lag in stages)
    total = n + deepest
    first = deepest + 2
    turns = max(0, (n - first) // 2)
    if turns < 2:
        turns = 0

    def one(s):
        for fn, lag in stages:
            b = s - lag
            if 0 <= b < n:
                fn(b, b % 2, b // 2)

    last = first + 2 * turns if turns else first
    for s in range(first):
        one(s)
    if turns:
        with eng.Fori(0, turns) as i:
            for d in range(2):
                for fn, lag in stages:
                    b = first + d - lag
                    fn(2 * i + b, b % 2, i + b // 2)
    for s in range(last, total):
        one(s)


def at(t, b):
    if isinstance(b, int):
        return t[:, b]
    ap = t[:, bass.ds(b, 1)]
    return ap.squeeze(1)


def cols(b, n):
    return bass.ds(b * n, n)


def free_after(eng, sem, b, per=1):
    if isinstance(b, int) and b < 2:
        return
    eng.wait_ge(sem, (b - 1) * per)


def build(nc, A, out):
    x_d = A["x"].rearrange("b s d -> s b d")
    ctx_d = A["ctx_1024"].rearrange("b s d -> s b d")
    NB, S, D = A["x"].shape
    KD = D // P
    NH0 = A["L0_xattn_igate_bias"].shape[0]
    DH0 = D // NH0
    FF = A["L0_ffn_w_gate"].shape[0]
    FT = FF // P
    DH1, NH1 = 16, D // 16
    NE = A["L1_ffn_w_router"].shape[1]
    NF = A["L1_ffn_wi"].shape[2]
    NFT = NF // P
    NG, CAP, TOPK = 2, 160, 2
    TG = NB // NG
    ROWS = NG * CAP
    SPARE = CAP - P
    SELW = P + NG * SPARE
    BLK = 32
    assert S == P and NB == 16 and D == 256

    ctx = ExitStack()
    with ctx:
        def sb(name, shape, dt=F32):
            return ctx.enter_context(nc.sbuf_tensor(name, shape, dt))

        def sem(name):
            return ctx.enter_context(nc.semaphore(name))

        RW = D + NE
        xr_d = nc.dram_tensor("token_rows", (NB * S, RW), F32, kind="Internal").ap()
        out_rows = out.rearrange("b s d -> (b s) d")

        ident = sb("ident", [P, P])
        ones = sb("ones", [P, P])
        tri = sb("tri", [P, P])
        stri = sb("stri", [P, P], BF16)
        onesb = sb("onesb", [P, P], BF16)
        cidx = sb("cidx", [P, SELW], BF16)
        ids = sb("ids", [P, 2 * NB + WIDE], BF16)
        pidx = sb("pidx", [P, 2], I32)
        par = sb("par", [P, 2])
        gb = sb("gb", [P, 2 * NH0])
        oscale = sb("oscale", [P, D])
        bv = sb("bv", [P, D])
        bo = sb("bo", [P, D])
        bq = sb("bq", [P, KD])
        bk = sb("bk", [P, KD])
        wrt_f = sb("wrt", [P, KD * NE + P])
        wrt = wrt_f[:, 0:KD * NE].rearrange("p (k e) -> p k e", k=KD)
        wT = [sb(f"wT{n}", [P, KD, D]) for n in range(4)]
        wupT = sb("wupT", [P, KD, FF])
        wgtT = sb("wgtT", [P, KD, FF])
        wdnT = sb("wdnT", [P, FT, D])
        X = sb("X", [P, NB, D])
        XIT = sb("XIT", [P, KD * NB * S])
        KT = sb("KT", [P, KD, NB * S])
        VW = NH1 * (DH1 + 1)
        Vf = sb("V", [P, NB * VW + WIDE])
        V = Vf[:, 0:NB * VW].rearrange("p (b h d) -> p b h d", b=NB, h=NH1)
        T = sb("T", [P, 2, D])
        XCT = sb("XCT", [P, 2, 4, P])
        Cu = sb("Cu", [P, 2, D])
        arena = sb("arena", [P, 2 * FT * NB * S])

        def view(o, *shape):
            n = int(np.prod(shape))
            names = "abcd"[:len(shape)]
            ap = arena[:, o:o + n]
            if len(shape) == 1:
                return ap
            kw = {names[k]: shape[k] for k in range(1, len(shape))}
            return ap.rearrange(f"p ({' '.join(names)}) -> p {' '.join(names)}", **kw)

        HALF = FT * NB * S
        U = view(0, FT, NB * S)
        G = view(HALF, FT, NB * S)
        HU = view(0, NB, NH0, DH0 + 1)
        H = view(4160, NB * NH0, DH0)
        HD = view(8256, 2, NH0, P)
        HC = view(9280, 2, NH0, P)
        VUW = NH0 * (DH0 + 1)
        VUf = view(11440, 2, VUW + DH0)
        VU = VUf[:, :, 0:VUW].rearrange("p u (h d) -> p u h d", h=NH0)
        XL = view(0, NB, D)
        CX = view(HALF, NB, D)
        WN = view(HALF + 4096, 3, 1536)
        LN = view(HALF + 4096 + 4608, 4, KD, D)
        KTf = KT[:, :, :].rearrange("p k n -> p (k n)")

        def tiles(buf, o, dt=F32):
            n = 2 * FT * P // (1 if dt == F32 else 2)
            v = buf[:, o * FT * P:o * FT * P + n]
            return (v if dt == F32 else v.bitcast(dt)).rearrange("p (u f n) -> p u f n", u=2, f=FT)
        SG = tiles(KTf, 0)
        SI = tiles(KTf, 2, U16)
        GI = tiles(KTf, 3, I16)
        OT = tiles(XIT, 0)
        G2 = tiles(XIT, 2, I16)
        UI = tiles(XIT, 3, I16)
        XITv = XIT[:, :].rearrange("p (k n) -> p k n", k=KD)
        PR = view(0, 2, NH1, P)
        PT = view(4096, 2, NH1, P)
        KM = view(8192, 2, KD, 2, P)
        QT = view(9216, 2, KD, P)
        AO = view(9728, 2, D)
        AT = view(10240, 2, KD, P)
        HT = view(0, 2, NFT, ROWS)
        XE = view(5120, 2, 3, RW)
        XET = view(6704, 2, KD, ROWS)
        YG = view(7984, 3, D)
        SEL = view(8752, 2 * NB * SELW // 2).bitcast(BF16).rearrange("p (u b c) -> p u b c", u=2, b=NB)
        XR = view(12160, NB, RW)
        WI = view(16384, 2, KD, NF)
        WO = view(20480, 2, NFT, D)

        wgate_f = view(12088, 6 * 2 * NH0 + P)
        wgate_g = wgate_f[:, 0:6 * 2 * NH0].rearrange("p (k g) -> p k g", k=6)

        ST = sb("ST", [P, NB * NH0, 6])
        mean = sb("mean", [P, NB * NH0])
        rstd = sb("rstd", [P, NB * NH0])
        s1 = sb("s1", [P, NB * NH0])
        s2 = sb("s2", [P, NB * NH0])
        s3 = sb("s3", [P, NB * NH0])
        var = sb("var", [P, NB * NH0])
        lnv = sb("lnv", [P, NB * NH0])
        yv = sb("yv", [P, NB * NH0])
        GA = view(HALF + 4096 + 4608 + 2048, NB, 2 * NH0)
        AG = sb("AG", [P, NB, 2 * NH0])
        MAu = sb("MAu", [P, 2, 2 * NH0])
        lf = view(11120, NB, NH0)
        az = view(11184, NB, NH0)
        ez = view(11248, NB, NH0)
        Acol = view(11312, NB, NH0)
        aT = view(10736, P)[0:NB * NH0]
        mT = view(10864, P)[0:NB * NH0]
        zT = view(10992, P)[0:NB * NH0]
        nm = sb("nm", [P, NB, NH0])
        nmx = view(11376, NB, NH0)
        den = sb("den", [P, 2, NB * NH0])
        am = sb("am", [P, 2, 24])
        gm = sb("gm", [P, 2])
        gr = sb("gr", [2, 2])
        gd = sb("gd", [2, 2])
        sc = sb("sc", [P, 24])
        wam, wsc, winv = (view(10304 + 144 * n, 3, 48) for n in range(3))
        rm = sb("rm", [P, 2, NH1])
        rs = sb("rs", [P, 2, NH1])
        LG = XR[:, :, D:]
        r1 = sb("r1", [P, NB])
        gates = sb("gates", [P, TOPK, NB])
        gcol = sb("gcol", [P, 2, 3])
        num = sb("num", [P, 2, 3])
        token = sb("token", [P, NE, 3], U32)
        RT = [XIT[:, 256 * n:256 * n + 256] for n in range(5)]
        OH, pos, tmp = (RT[n].rearrange("p (k b e) -> p k b e", k=TOPK, b=NB) for n in (0, 1, 2))
        tot, inc = (RT[n].rearrange("p (g e k t) -> p g e k t", g=NG, e=NE, k=TOPK) for n in (3, 4))
        q1 = XIT[:, 1280:1408].rearrange("p (b e) -> p b e", b=NB)
        rank8 = XIT[:, 1408:1536].rearrange("p (b e) -> p b e", b=NB)
        place = XIT[:, 1536:1664].rearrange("p (b e) -> p b e", b=NB)
        shift = XIT[:, 1664:1792].rearrange("p (b e) -> p b e", b=NB)
        segm = XIT[:, 1792:2048]
        OHb = XIT[:, 2048:2176].bitcast(BF16)
        placeb = XIT[:, 2176:2240].bitcast(BF16).rearrange("p (b e) -> p b e", b=NB)
        LW = XIT[:, 2240:2368].rearrange("p (b e) -> p b e", b=NB)
        cidx_f = XIT[:, 2368:2368 + SELW]
        ids_f = XIT[:, 2560:2560 + 2 * NB].rearrange("p (b c) -> p b c", b=NB)

        pA = ctx.enter_context(nc.psum_tensor("pA", [P, 4, 512], F32))
        pB = ctx.enter_context(nc.psum_tensor("pB", [P, 2, 512], F32))
        pC = ctx.enter_context(nc.psum_tensor("pC", [P, 2, 512], F32))
        ps = [pA[:, i, :] for i in range(4)] + [pB[:, i, :] for i in range(2)] + [pC[:, i, :] for i in range(2)]
        S_ = {}

        class Sems:

            def __getitem__(self, name):
                if name not in S_:
                    S_[name] = sem(name)
                return S_[name]

        s = Sems()
        block = ctx.enter_context(nc.Block())

        def chain(eng, name):
            count = [0]

            def link(ins):
                count[0] += 1
                ins.then_inc(s[name], 1)
                eng.wait_ge(s[name], count[0])
            return link

        XQ = 4
        WB = 3 * 48 // NB
        W1 = NB - 4

        def W_b(b):
            return WN[:, :, :].rearrange("p m (k c) -> p (m k) c", c=BLK)[:, cols(b, WB), :]

        def S_b(t, b):
            return t[:, :, :].rearrange("p m k -> p (m k)")[:, cols(b, WB)]

        def H_b(b):
            return H[:, cols(b, NH0), :].rearrange("p h d -> p (h d)")

        def F_b(t, b):
            return t[:, :, cols(b, P)]

        @block.sync
        def _(sp):
            def bcast(dst, src):
                sp.dma_start(dst, src.partition_broadcast(P)).then_inc(s["small_in"], 16)

            def late(dst, src):
                sp.dma_start(dst, src.partition_broadcast(P)).then_inc(s["late_in"], 16)

            def quarter(dst, src, q, name):
                sp.dma_start(dst[:, 4 * q:4 * q + 4, :], src[:, 4 * q:4 * q + 4, :]).then_inc(s[name], 16)
            for q in range(XQ):
                quarter(X, x_d, q, f"x_in{q}")
            gk = wgate_g
            sp.dma_start(gk[:, :, 0:NH0], A["L0_xattn_igate_kernel"].rearrange("(k p) h -> p k h", p=P)).then_inc(s["small_in"], 16)
            sp.dma_start(gk[:, :, NH0:], A["L0_xattn_fgate_kernel"].rearrange("(k p) h -> p k h", p=P)).then_inc(s["small_in"], 16)
            bcast(gb[:, 0:NH0], A["L0_xattn_igate_bias"])
            bcast(gb[:, NH0:], A["L0_xattn_fgate_bias"])
            quarter(CX, ctx_d, 0, "c_in0")
            quarter(CX, ctx_d, 1, "c_in1")
            quarter(CX, ctx_d, 2, "c_in2")
            quarter(CX, ctx_d, 3, "c_in3")
            sp.dma_start(WN[:, 0, :].rearrange("p (t d) -> p t d", t=FT), A["L0_ffn_w_up"].rearrange("(t p) d -> p t d", p=P)).then_inc(s["wbig_in"], 16)
            sp.dma_start(WN[:, 1, :].rearrange("p (t d) -> p t d", t=FT), A["L0_ffn_w_gate"].rearrange("(t p) d -> p t d", p=P)).then_inc(s["wbig_in"], 16)
            sp.dma_start(WN[:, 2, :].rearrange("p (t d) -> p t d", t=KD), A["L0_ffn_w_down"].rearrange("(t p) d -> p t d", p=P)).then_inc(s["wbig_in"], 16)
            late(oscale[:, :], A["L0_xattn_outnorm_scale"])
            late(bv[:, :], A["L1_xattn_b_v"])
            late(bo[:, :], A["L1_xattn_b_o"])
            sp.dma_start(bk[:, :], A["L1_xattn_b_k"].rearrange("(k p) -> p k", p=P), allow_slow_non_contiguous=True).then_inc(s["late_in"], 16)
            sp.dma_start(bq[:, :], A["L1_xattn_b_q"].rearrange("(k p) -> p k", p=P), allow_slow_non_contiguous=True).then_inc(s["late_in"], 16)
            sp.dma_start(wrt[:, :, :], A["L1_ffn_w_router"].rearrange("(k p) e -> p k e", p=P)).then_inc(s["late_in"], 16)
            for n, nme in ((1, "k"), (2, "v"), (0, "q"), (3, "o")):
                sp.dma_start(LN[:, n], A[f"L1_xattn_w_{nme}"].rearrange("(k p) d -> p k d", p=P)).then_inc(s[f"w{nme}_in"], 16)


            def ctx_again(b, u, h):
                if isinstance(b, int) and b < 2:
                    sp.wait_ge(s["tr2_done"], NB)
                free_after(sp, s["tr4_done"], b)
                sp.dma_start(Cu[:, u, :], at(ctx_d, b)).then_inc(s[f"ctx_in{u}"], 16)
            steps(sp, NB, [(ctx_again, 0)])

            def weights_in(e, u, h):
                if isinstance(e, int) and e < 2:
                    sp.wait_ge(s["gm_ready"], 4)
                free_after(sp, s["h_done"], e, NFT)
                sp.dma_start(WI[:, u], A["L1_ffn_wi"][bass.ds(e, 1)].squeeze(0).rearrange("(k p) f -> p k f", p=P)).then_inc(s[f"wi_in{u}"], 16)

            def weights_out(e, u, h):
                free_after(sp, s["ec_done"], e, 3)
                sp.dma_start(WO[:, u], A["L1_ffn_wo"][bass.ds(e, 1)].squeeze(0).rearrange("(k p) f -> p k f", p=P)).then_inc(s[f"wo_in{u}"], 16)
            weights_in(0, 0, 0)
            weights_out(0, 0, 0)
            weights_in(1, 1, 0)
            weights_out(1, 1, 0)
            for q in range(XQ):
                sp.wait_ge(s["x3_ready"], 4 * q + 4)
                sp.dma_start(out.rearrange("b s d -> s b d")[:, 4 * q:4 * q + 4, :], X[:, 4 * q:4 * q + 4, :]).then_inc(s["x3_out"], 16)
            xr = xr_d.rearrange("(b p) d -> p b d", p=P)
            for q in range(XQ):
                sp.wait_ge(s["xr_ready"], 2 * q + 2)
                sp.dma_start(xr[:, 4 * q:4 * q + 4, 0:D], XR[:, 4 * q:4 * q + 4, 0:D]).then_inc(s["xr_out"], 16)
            sp.wait_ge(s["probs"], 1)
            sp.dma_start(xr[:, :, D:], LG[:, :, :]).then_inc(s["xr_out"], 16)

            def both(e, u, h):
                if isinstance(e, int) and e < 2:
                    return
                weights_in(e, u, h)
                weights_out(e, u, h)
            steps(sp, NE, [(both, 0)])
            sp.wait_ge(s["rows_out"], 16 * 3 * NE)
            sp.wait_ge(s["x3_out"], 16 * XQ)

        @block.gpsimd
        def _(pool):
            link = chain(pool, "pool_chain")
            nc.gpsimd.memset(ones[:, :], 1.0)
            nc.gpsimd.memset(onesb[:, :], 1.0)
            nc.gpsimd.memset(ids[:, :], 0.0)
            nc.gpsimd.memset(zT[:, :], 0.0)
            nc.gpsimd.memset(V[:, :, :, DH1:], 1.0)
            nc.gpsimd.memset(Vf[:, NB * VW:], 0.0)
            nc.gpsimd.memset(wgate_f[:, 6 * 2 * NH0:], 0.0)
            nc.gpsimd.memset(wrt_f[:, KD * NE:], 0.0)
            nc.gpsimd.memset(VU[:, :, :, DH0:], 1.0)
            nc.gpsimd.memset(VUf[:, :, VUW:], 0.0)
            link(nc.gpsimd.memset(ident[:, :], 0.0))
            nc.gpsimd.affine_select(out=ident[:, :], in_=ident[:, :], compare_op=ALU.not_equal, fill=1.0,
                                    base=0, pattern=[[-1, P]], channel_multiplier=1)
            nc.gpsimd.affine_select(out=tri[:, :], in_=ones[:, :], compare_op=ALU.is_ge, fill=0.0,
                                    base=0, pattern=[[1, P]], channel_multiplier=-1)
            nc.gpsimd.affine_select(out=stri[:, :], in_=onesb[:, :], compare_op=ALU.is_gt, fill=0.0,
                                    base=0, pattern=[[1, P]], channel_multiplier=-1)
            nc.gpsimd.iota(pidx[:, 0:1], pattern=[[0, 1]], base=0, channel_multiplier=1).then_inc(s["consts"], 1)

            def w_scale(b, u, h):
                pool.wait_ge(s["w_step"], 5 * b + 5)
                nc.gpsimd.tensor_tensor(W_b(b), W_b(b), S_b(wsc, b).unsqueeze(2).broadcast_to([P, WB, BLK]), ALU.mult).then_inc(s["w_q"], 1)
            steps(pool, W1, [(w_scale, 0)])

            def causal(b, u, h):
                pool.wait_ge(s["c_ready"], b + 1)
                nc.gpsimd.tensor_tensor(HC[:, u], HC[:, u], tri[:, :].unsqueeze(1).broadcast_to([P, NH0, P]), ALU.mult).then_inc(s["c_masked"], 1)

            def copy_v(b, u, h):
                free_after(pool, s["av_done"], b)
                c = at(CX, b).rearrange("p (h d) -> p h d", h=NH0)
                nc.gpsimd.tensor_tensor(VU[:, u, :, 0:DH0], c, ones[:, 0:DH0].unsqueeze(1).broadcast_to([P, NH0, DH0]), ALU.mult).then_inc(s["v_copied"], 1)
            for q in range(XQ):
                pool.wait_ge(s[f"c_in{q}"], 16)
            steps(pool, NB, [(copy_v, 0), (causal, 0)])
            for b in range(W1, NB):
                w_scale(b, b % 2, b // 2)
            pool.wait_ge(s["late_in"], 16 * 6)

            def h_scale(b, u, h):
                pool.wait_ge(s["h_normed"], b + 1)
                pool.wait_ge(s["last_normed"], b + 1)
                nc.gpsimd.tensor_tensor(H_b(b), H_b(b), oscale[:, :], ALU.mult).then_inc(s["h_scaled"], 1)
            steps(pool, NB, [(h_scale, 0)])

            def v_bias(b, u, h):
                pool.wait_ge(s["kv_copied"], b + 1)
                v = at(V, b)[:, :, 0:DH1]
                nc.gpsimd.tensor_tensor(v, v, bv[:, :].rearrange("p (h d) -> p h d", h=NH1), ALU.add).then_inc(s["v_biased"], 1)
            steps(pool, NB, [(v_bias, 0)])

            def split_keys(b, u, h):
                if isinstance(b, int) and b == 0:
                    pool.wait_ge(s["down_done"], NB)
                free_after(pool, s["scores"], b)
                for r in range(2):
                    last = nc.gpsimd.tensor_tensor(KM[:, u, :, r, :], KT[:, :, cols(b, P)], par[:, r:r + 1].unsqueeze(2).broadcast_to([P, KD, P]), ALU.mult)
                last.then_inc(s["km_ready"], 1)

            def add_bo(b, u, h):
                pool.wait_ge(s["xn3"], b + 1)
                nc.gpsimd.tensor_tensor(at(X, b), at(X, b), bo[:, :], ALU.add).then_inc(s["bo_added"], 1)
            steps(pool, NB, [(split_keys, 0), (add_bo, 0)])

            nc.gpsimd.iota(rank8[:, :, :], pattern=[[0, NB], [-1, NE]], base=NE, channel_multiplier=0,
                           allow_small_or_imprecise_dtypes=True)
            nc.gpsimd.iota(cidx_f, pattern=[[1, SELW]], base=1, channel_multiplier=0, allow_small_or_imprecise_dtypes=True)
            nc.gpsimd.iota(ids_f[:, :, 0], pattern=[[P, NB]], base=-NB * P, channel_multiplier=0, allow_small_or_imprecise_dtypes=True)
            nc.gpsimd.iota(ids_f[:, :, 1], pattern=[[0, NB]], base=0, channel_multiplier=1, allow_small_or_imprecise_dtypes=True)
            pool.wait_ge(s["o_done"], NB)
            nc.gpsimd.memset(XE[:, :, :, :], 0.0)
            nc.gpsimd.memset(YG[:, :, :], 0.0)
            link(nc.gpsimd.iota(segm[:, :], pattern=[[0, NG * NE], [1, TOPK * TG]], base=0,
                                channel_multiplier=0, allow_small_or_imprecise_dtypes=True))
            nc.gpsimd.tensor_scalar(segm[:, :], segm[:, :], 1.0, None, ALU.min).then_inc(s["tables"], 1)

            def indirect(e, c, dram, sbuf, gather):
                n = P if c < 2 else ROWS - 2 * P
                where = bass.IndirectOffsetOnAxis(ap=token[0:n, e, c:c + 1], axis=0)
                if gather:
                    return nc.gpsimd.indirect_dma_start(out=sbuf[0:n, c, :], out_offset=None, in_=dram, in_offset=where,
                                                        bounds_check=NB * S - 1, oob_is_err=False)
                return nc.gpsimd.indirect_dma_start(out=dram, out_offset=where, in_=sbuf[0:n, c, :], in_offset=None,
                                                    bounds_check=NB * S - 1, oob_is_err=False)
            pool.wait_ge(s["xr_out"], 16 * (XQ + 1))
            pool.wait_ge(s["x3_out"], 16 * XQ)
            for t in range(NE + 3):
                if t < NE:
                    pool.wait_ge(s["token_ready"], t + 1)
                    if t >= 2:
                        pool.wait_ge(s["xe_tr"], t - 1)
                        pool.wait_ge(s["gcol_ready"], t - 1)
                    for c in range(3):
                        indirect(t, c, xr_d, XE[:, t % 2], True).then_inc(s[f"xe_in{t % 2}"], 16)
                e = t - 3
                if e >= 0:
                    if e >= 1:
                        pool.wait_ge(s["rows_out"], 16 * 3 * e)
                    for c in range(3):
                        indirect(e, c, out_rows, YG, True).then_inc(s["yg_in"], 16)
                    for c in range(3):
                        pool.wait_ge(s["y_ready"], 3 * e + c + 1)
                        indirect(e, c, out_rows, YG, False).then_inc(s["rows_out"], 16)

        @block.scalar
        def _(act):
            link = chain(act, "act_chain")

            def rsqrt(k, n):
                act.wait_ge(s["ln_var"], k + 1)
                link(nc.scalar.activation(lnv[:, 0:n], var[:, 0:n], ACT.Ln))
                nc.scalar.activation(yv[:, 0:n], lnv[:, 0:n], ACT.Exp, scale=-0.5).then_inc(s["ln_y"], 1)

            rsqrt(0, NB)

            def copy_t(b, u, h):
                act.wait_ge(s["tr_done"], b + 1)
                free_after(act, s["g_done"], b)
                nc.scalar.activation(XCT[:, u], ps[u][:, :].rearrange("p (k n) -> p k n", k=4), ACT.Copy).then_inc(s["xct_ready"], 1)

            steps(act, NB, [(copy_t, 0)])
            act.wait_ge(s["fgate_dve"], 1)
            link(nc.scalar.activation(ez[:, :, :], az[:, :, :], ACT.Exp, scale=-1.0))
            nc.scalar.activation(ez[:, :, :], ez[:, :, :], ACT.Ln, bias=1.0).then_inc(s["fgate_act"], 1)
            act.wait_ge(s["fgate_dve"], 5)
            nc.scalar.activation(nm[:, :, :], nmx[:, :, :], ACT.Exp, scale=-1.0).then_inc(s["fgate_act"], 1)

            def decay(b, u, h):
                act.wait_ge(s["mb_done"], b + 1)
                free_after(act, s["c_ready"], b)
                for n in range(NH0):
                    last = nc.scalar.activation(HD[:, u, 2 * (n % 2) + n // 2, :], ps[2 + u][:, n * P:(n + 1) * P], ACT.Exp,
                                                bias=MAu[:, u, NH0 + n:NH0 + n + 1], scale=-1.0)
                last.then_inc(s["decay"], 1)

            def copy_u(b, u, h):
                act.wait_ge(s["av_done"], b + 1)
                nc.scalar.activation(at(HU, b), pC[:, u, 0:NH0 * (DH0 + 1)].rearrange("p (h d) -> p h d", h=NH0), ACT.Copy).then_inc(s["u_copied"], 1)
            steps(act, NB, [(decay, 0), (copy_u, 2)])
            rsqrt(1, NB * NH0)
            act.wait_ge(s["head_stat"], 1)

            def head_norm(b, u, h):
                for n in range(NH0 - 1):
                    last = nc.scalar.activation(H[:, cols(b * NH0 + n, 1), :].squeeze(1), at(HU, b)[:, n, 0:DH0], ACT.Identity, scale=rstd[:, cols(b * NH0 + n, 1)], bias=s2[:, cols(b * NH0 + n, 1)])
                last.then_inc(s["h_normed"], 1)
            steps(act, NB, [(head_norm, 0)])
            rsqrt(2, NB)
            for n in range(13):
                if n < 9:
                    dst = (wupT, wgtT)[n // 3][:, :, :].rearrange("p k (g c) -> p k g c", g=3)[:, :, n % 3, :] if n < 6 else \
                        wdnT[:, 2 * (n - 6):2 * (n - 6) + 2, :]
                else:
                    dst = wT[n - 9][:, :, :]
                act.wait_ge(s["wtr_done"], n + 1)
                nc.scalar.activation(dst, ps[2 + n % 2][:, :].rearrange("p (k c) -> p k c", k=2), ACT.Copy).then_inc(s["wtr_copied"], 1)

            def copy_x(b, u, h):
                act.wait_ge(s["tr3_done"], b + 1)
                nc.scalar.activation(XITv[:, :, cols(b, P)], ps[u][:, 0:2 * P].rearrange("p (k n) -> p k n", k=2), ACT.Copy).then_inc(s["xit_ready"], 1)

            def evacuate(dst, name, c, f):
                act.wait_ge(s[f"{name}_done"], c * FT + f + 1)
                nc.scalar.activation(dst[:, f, cols(c, 512)], ps[2 + f][:, :], ACT.Copy).then_inc(s[f"{name}_out"], 1)

            def gate_chunk(c):
                for f in range(FT):
                    evacuate(G, "gate", c, f)
                    if f < 4 and not (isinstance(c, int) and c == 3):
                        copy_x(4 * c + 4 + f, f % 2, 0)
            for j in range(4):
                copy_x(j, j % 2, 0)
            gate_chunk(0)
            with act.Fori(1, 3) as c:
                gate_chunk(c)
            gate_chunk(3)
            act.wait_ge(s["sc_gate"], 1)

            def g_to_int(b, u):
                free_after(act, s["gs_done"], b)
                nc.scalar.activation(GI[:, u], F_b(G, b), ACT.Copy, scale=sc[:, 7:8]).then_inc(s["g_int0"], 1)

            def up_chunk(c):
                for f in range(FT):
                    if f >= 4:
                        evacuate(U, "up", c, f)
                        continue
                    b, u = 4 * c + f, f % 2
                    early = isinstance(c, int) and c == 0 and f < 2
                    act.wait_ge(s[f"g_int{u}"], 2 * c + f // 2 + 1)
                    if not early:
                        act.wait_ge(s["sig_int"], b - 1)
                    nc.scalar.activation(SG[:, u], GI[:, u], ACT.Sigmoid, scale=sc[:, 5:6]).then_inc(s["sig"], 1)
                    evacuate(U, "up", c, f)
                    if not early:
                        act.wait_ge(s["gs_done"], b - 1)
                    act.wait_ge(s["sig"], b + 1)
                    nc.scalar.activation(SI[:, u], SG[:, u], ACT.Copy, scale=65536.0).then_inc(s["sig_int"], 1)
                    if u == 1 and not (isinstance(c, int) and c == 3 and f == 3):
                        g_to_int(b + 1, 1 - u)
            g_to_int(0, 0)
            up_chunk(0)
            with act.Fori(1, 3) as c:
                up_chunk(c)
            up_chunk(3)
            act.wait_ge(s["sc_up"], 1)

            def up_int(b, u, h):
                free_after(act, s["prod"], b)
                nc.scalar.activation(UI[:, u], F_b(U, b), ACT.Copy, scale=sc[:, 6:7]).then_inc(s["u_int"], 1)

            def copy_c4(b, u, h):
                act.wait_ge(s["tr4_done"], b + 1)
                free_after(act, s["kv_done"], b)
                nc.scalar.activation(XCT[:, u, 2:4], ps[u][:, 0:2 * P].rearrange("p (k n) -> p k n", k=2), ACT.Copy).then_inc(s["xct4_ready"], 1)

            def keys_values(b, u, h):
                act.wait_ge(s["kv_done"], b + 1)
                for k in range(KD):
                    nc.scalar.activation(KT[:, k, cols(b, P)], ps[2 + u][:, k * P:(k + 1) * P], ACT.Identity, bias=bk[:, k:k + 1])
                nc.scalar.activation(at(V, b)[:, :, 0:DH1], ps[2 + u][:, 2 * P:4 * P].rearrange("p (h d) -> p h d", h=NH1), ACT.Copy).then_inc(s["kv_copied"], 1)
            act.wait_ge(s["late_in"], 16 * 6)
            steps(act, NB, [(copy_c4, 0), (up_int, 0), (keys_values, 1)])
            rsqrt(3, NB)

            def xt_copy(b, u, h):
                act.wait_ge(s["c_tr"], b + 1)
                free_after(act, s["c_q"], b)
                nc.scalar.activation(XCT[:, u, 0:2], ps[4][:, 0:2 * P].rearrange("p (k n) -> p k n", k=2), ACT.Copy).then_inc(s["c_xt"], 1)

            def q_out(b, u, h):
                act.wait_ge(s["c_q"], b + 1)
                free_after(act, s["scores"], b)
                for k in range(KD):
                    last = nc.scalar.activation(QT[:, u, k, :], ps[4][:, (2 + k) * P:(3 + k) * P], ACT.Identity, scale=0.25, bias=bq[:, k:k + 1])
                last.then_inc(s["qt_ready"], 1)

            def exps(b, u, h):
                for e in range(2):
                    act.wait_ge(s["s_sub"], 2 * b + e + 1)
                    part = PR[:, u, e * NH1 // 2:(e + 1) * NH1 // 2, :]
                    nc.scalar.activation(part, part, ACT.Exp).then_inc(s["p_ready"], 1)

            def pt_copy(b, u, groups):
                for g in groups:
                    act.wait_ge(s["pt_tr"], b * 4 + g + 1)
                    nc.scalar.activation(PT[:, u, 4 * g:4 * g + 4, :], pC[:, g % 2, :].rearrange("p (k n) -> p k n", k=4), ACT.Copy).then_inc(s["pt_ready"], 1)

            def pt_first(b, u, h):
                free_after(act, s["pv_done"], b)
                pt_copy(b, u, (0, 1))

            def pt_third(b, u, h):
                pt_copy(b, u, (2,))

            def pt_last(b, u, h):
                pt_copy(b, u, (3,))

            def at_copy(b, u, h):
                act.wait_ge(s["a_tr"], b + 1)
                free_after(act, s["o_done"], b)
                nc.scalar.activation(AT[:, u], ps[4][:, 0:2 * P].rearrange("p (k n) -> p k n", k=2), ACT.Copy).then_inc(s["at_ready"], 1)
            steps(act, NB, [(exps, 2), (xt_copy, 0), (pt_first, 2), (q_out, 0), (pt_third, 2), (at_copy, 3), (pt_last, 2)])
            rsqrt(4, NB)

            def xt4(c, u, h):
                act.wait_ge(s["d_tr"], c + 1)
                free_after(act, s["d_lg"], c)
                nc.scalar.activation(XCT[:, u], ps[u][:, :].rearrange("p (k n) -> p k n", k=4), ACT.Copy).then_inc(s["d_xt"], 1)
            steps(act, NB // 2, [(xt4, 0)])
            act.wait_ge(s["lg_sub"], 1)
            nc.scalar.activation(LG[:, :, :], LG[:, :, :], ACT.Exp).then_inc(s["lg_exp"], 1)

            def xet(e, u, h):
                act.wait_ge(s["xe_tr"], e + 1)
                free_after(act, s["h_done"], e, NFT)
                for k in range(KD):
                    last = nc.scalar.activation(XET[:, u, k, :], ps[k][:, 0:ROWS], ACT.Copy)
                last.then_inc(s["xet_ready"], 1)

            def relu(e, u, h):
                free_after(act, s["ec_done"], e, 3)
                for f in range(NFT):
                    act.wait_ge(s["h_done"], e * NFT + f + 1)
                    nc.scalar.activation(HT[:, u, f, :], ps[2 + f % 2][:, 0:ROWS], ACT.Relu).then_inc(s["h_relu"], 1)
            steps(act, NE, [(relu, 1), (xet, 0)])

        @block.vector
        def _(dve):
            link = chain(dve, "dve_chain")
            V_ = nc.vector

            def moments(k, n, N, factor=None):
                st = ST[:, 0:n, :]
                m0, m1, v0, v1 = (st[:, :, c] for c in (1, 4, 2, 5))
                V_.tensor_tensor(s1[:, 0:n], m0, m1, ALU.add)
                V_.tensor_tensor(s3[:, 0:n], v0, v1, ALU.add)
                link(V_.tensor_tensor(s2[:, 0:n], m0, m1, ALU.subtract))
                V_.tensor_scalar(mean[:, 0:n], s1[:, 0:n], 0.5, None, ALU.mult)
                V_.tensor_scalar(s3[:, 0:n], s3[:, 0:n], 1.0 / N, EPS if factor is None else 0.0, ALU.mult, ALU.add)
                link(V_.scalar_tensor_tensor(out=lnv[:, 0:n], in0=s2[:, 0:n], scalar=0.25, in1=s2[:, 0:n], op0=ALU.mult, op1=ALU.mult))
                if factor is None:
                    V_.tensor_tensor(var[:, 0:n], s3[:, 0:n], lnv[:, 0:n], ALU.add).then_inc(s["ln_var"], 1)
                else:
                    link(V_.tensor_tensor(s1[:, 0:n], s3[:, 0:n], lnv[:, 0:n], ALU.add))
                    link(V_.tensor_tensor(s1[:, 0:n], s1[:, 0:n], factor, ALU.mult))
                    link(V_.tensor_tensor(s1[:, 0:n], s1[:, 0:n], factor, ALU.mult))
                    V_.tensor_scalar(var[:, 0:n], s1[:, 0:n], EPS, None, ALU.add).then_inc(s["ln_var"], 1)
                dve.wait_ge(s["ln_y"], k + 1)
                link(V_.tensor_tensor(s1[:, 0:n], yv[:, 0:n], yv[:, 0:n], ALU.mult))
                link(V_.tensor_tensor(s1[:, 0:n], s1[:, 0:n], var[:, 0:n], ALU.mult))
                link(V_.tensor_scalar(s1[:, 0:n], s1[:, 0:n], -0.5, 1.5, ALU.mult, ALU.add))
                link(V_.tensor_tensor(rstd[:, 0:n], s1[:, 0:n], yv[:, 0:n], ALU.mult))
                if factor is not None:
                    link(V_.tensor_tensor(rstd[:, 0:n], rstd[:, 0:n], factor, ALU.mult))

            def normed(dst, b):
                return V_.tensor_scalar(dst, at(X, b), mean[:, cols(b, 1)], rstd[:, cols(b, 1)], ALU.subtract, ALU.mult)

            dve.wait_ge(s["consts"], 1)
            link(V_.tensor_scalar(pidx[:, 1:2], pidx[:, 0:1], 16, None, ALU.bitwise_and))
            V_.tensor_scalar(par[:, 0:1], pidx[:, 1:2], 0.0, None, ALU.is_equal)
            link(V_.tensor_scalar(par[:, 1:2], pidx[:, 1:2], 0.0, None, ALU.is_gt))

            for q in range(XQ):
                dve.wait_ge(s[f"x_in{q}"], 16)
                for b in range(4 * q, 4 * q + 4):
                    last = V_.bn_stats(ST[:, b, :], X[:, b, :])
            link(last)
            moments(0, NB, D)
            dve.wait_ge(s["small_in"], 16 * 4)
            V_.tensor_tensor(wgate_g[:, 2:4, :], wgate_g[:, 2:4, :], wgate_g[:, 4:6, :], ALU.add).then_inc(s["gw_ready"], 1)

            def copy_ctx(b, u, h):
                if isinstance(b, int) and b == 0:
                    dve.wait_ge(s["c_in0"], 16)
                if isinstance(b, int) and b == 4:
                    for q in range(1, XQ):
                        dve.wait_ge(s[f"c_in{q}"], 16)
                free_after(dve, s["tr_done"], b)
                V_.tensor_copy(Cu[:, u, :], at(CX, b))

            def norm1(b, u, h):
                normed(T[:, u, :], b).then_inc(s["xln_ready"], 1)

            def w_max(b, u, h):
                if isinstance(b, int) and b == 0:
                    dve.wait_ge(s["wbig_in"], 16 * 3)
                V_.tensor_reduce(S_b(wam, b), W_b(b), AX.X, ALU.max, apply_absolute_value=True).then_inc(s["w_step"], 1)

            def w_scale(b, u, h):
                dve.wait_ge(s["w_step"], 5 * b + 1)
                V_.tensor_scalar(S_b(wsc, b), S_b(wam, b), 1.0 / 7.0, TINY, ALU.mult, ALU.max).then_inc(s["w_step"], 1)

            def w_round(b, u, h):
                w, in_ = W_b(b), S_b(winv, b)
                dve.wait_ge(s["w_step"], 5 * b + 2)
                V_.reciprocal(in_, S_b(wsc, b)).then_inc(s["w_step"], 1)
                dve.wait_ge(s["w_step"], 5 * b + 3)
                V_.tensor_tensor(w, w, in_.unsqueeze(2).broadcast_to([P, WB, BLK]), ALU.mult).then_inc(s["w_step"], 1)
                dve.wait_ge(s["w_step"], 5 * b + 4)
                V_.tensor_scalar(w, w, ROUND, -ROUND, ALU.add, ALU.add).then_inc(s["w_step"], 1)

            def first_part(fn):
                return lambda b, u, h: None if isinstance(b, int) and b >= W1 else fn(b, u, h)
            steps(dve, NB, [(first_part(w_max), 5), (copy_ctx, 0), (first_part(w_scale), 5), (norm1, 0), (first_part(w_round), 5)])
            dve.wait_ge(s["g_done"], NB)
            V_.tensor_tensor(GA[:, :, :], ps[6][:, 0:NB * 2 * NH0].rearrange("p (b g) -> p b g", b=NB), gb[:, :].unsqueeze(1).broadcast_to([P, NB, 2 * NH0]),
                             ALU.add).then_inc(s["ga_ready"], 1)
            dve.wait_ge(s["ga_ready"], 1)

            fg, ig = GA[:, :, NH0:], GA[:, :, 0:NH0]
            V_.scalar_tensor_tensor(out=az[:, :, :], in0=fg, scalar=-1.0, in1=fg, op0=ALU.mult, op1=ALU.max).then_inc(s["fgate_dve"], 1)
            link(V_.tensor_scalar(lf[:, :, :], fg, 0.0, None, ALU.min))
            dve.wait_ge(s["fgate_act"], 1)
            V_.tensor_tensor(lf[:, :, :], lf[:, :, :], ez[:, :, :], ALU.subtract).then_inc(s["fgate_dve"], 1)
            dve.wait_ge(s["fgate_pe"], 1)
            cs = ps[7][:, 256:256 + NB * NH0].rearrange("p (b h) -> p b h", h=NH0)
            V_.tensor_tensor(AG[:, :, NH0:], ig, cs, ALU.subtract)
            V_.tensor_tensor(Acol[:, :, :], ig, cs, ALU.subtract).then_inc(s["fgate_dve"], 1)
            dve.wait_ge(s["fgate_pe"], 2)
            link(V_.tensor_copy(aT[:, :], ps[7][0:NB * NH0, 0:P]))
            V_.tensor_tensor_scan(mT[:, :], zT[:, :], aT[:, :], -3e38, ALU.add, ALU.max).then_inc(s["fgate_dve"], 1)
            dve.wait_ge(s["fgate_pe"], 3)
            mcol = ps[7][:, P:P + NB * NH0].rearrange("p (b h) -> p b h", h=NH0)
            link(V_.tensor_copy(AG[:, :, 0:NH0], mcol))
            V_.tensor_tensor(nmx[:, :, :], cs, AG[:, :, 0:NH0], ALU.add).then_inc(s["fgate_dve"], 1)

            def norm2(b, u, h):
                free_after(dve, s["tr2_done"], b)
                free_after(dve, s["decay"], b)
                free_after(dve, s["mb_done"], b)
                V_.tensor_copy(MAu[:, u, :], at(AG, b))
                V_.tensor_copy(Cu[:, u, :], at(CX, b))
                normed(T[:, u, :], b).then_inc(s["xln2_ready"], 1)

            def copy_c(b, u, h):
                dve.wait_ge(s["tr2_done"], b + 1)
                free_after(dve, s["qk_done"], b)
                if isinstance(b, int) and b < 2:
                    dve.wait_ge(s["g_done"], NB)
                V_.tensor_scalar(XCT[:, u, 0:2], ps[u][:, 0:2 * P].rearrange("p (k n) -> p k n", k=2), 0.125, None, ALU.mult)
                V_.tensor_copy(XCT[:, u, 2:4], ps[u][:, 2 * P:4 * P].rearrange("p (k n) -> p k n", k=2)).then_inc(s["c_copied"], 1)

            def weigh(b, u, h):
                dve.wait_ge(s["qk_done"], b + 1)
                dve.wait_ge(s["decay"], b + 1)
                free_after(dve, s["av_done"], b)
                V_.scalar_tensor_tensor(out=HC[:, u].rearrange("p (r k) n -> p r (k n)", r=2), in0=HD[:, u].rearrange("p (r k) n -> p r (k n)", r=2),
                                        scalar=1.0, in1=pB[:, :, 0:2 * P], op0=ALU.min, op1=ALU.mult).then_inc(s["c_ready"], 1)

            def head_stats(b, u, h):
                dve.wait_ge(s["u_copied"], b + 1)
                for n in range(NH0):
                    last = V_.bn_stats(ST[:, cols(b * NH0 + n, 1), :].squeeze(1), at(HU, b)[:, n, 0:DH0])
                last.then_inc(s["hst"], 1)

            def weights_rest(b, u, h):
                if isinstance(b, int) and b < NB - W1:
                    w_max(W1 + b, u, h)
                    w_scale(W1 + b, u, h)
                    w_round(W1 + b, u, h)
            steps(dve, NB, [(weights_rest, 1), (copy_c, 1), (norm2, 0), (weigh, 2), (head_stats, 4)])
            dve.wait_ge(s["hst"], NB)
            dve.wait_ge(s["fgate_act"], 2)
            dve.wait_ge(s["u_copied"], NB)
            d = [den[:, n, :].rearrange("p (b h) -> p b h", h=NH0) for n in range(2)]
            rowsum = HU[:, :, :, DH0]
            link(V_.scalar_tensor_tensor(out=d[0], in0=rowsum, scalar=-1.0, in1=rowsum, op0=ALU.mult, op1=ALU.max))
            link(V_.tensor_tensor(d[1], d[0], nm[:, :, :], ALU.max))
            link(V_.tensor_scalar(d[0], d[1], 1e-6, None, ALU.add))
            link(V_.reciprocal(d[1], d[0]))
            moments(1, NB * NH0, DH0, den[:, 1, :])
            V_.scalar_tensor_tensor(out=s2[:, :], in0=mean[:, :], scalar=-1.0, in1=rstd[:, :], op0=ALU.mult, op1=ALU.mult).then_inc(s["head_stat"], 1)

            def last_head(b, u, h):
                V_.tensor_scalar(H[:, cols(b * NH0 + NH0 - 1, 1), :].squeeze(1), at(HU, b)[:, NH0 - 1, 0:DH0], mean[:, cols(b * NH0 + NH0 - 1, 1)], rstd[:, cols(b * NH0 + NH0 - 1, 1)], ALU.subtract, ALU.mult).then_inc(s["last_normed"], 1)

            def add_heads(b, u, h):
                dve.wait_ge(s["h_scaled"], b + 1)
                V_.tensor_tensor(at(X, b), at(X, b), H_b(b), ALU.add).then_inc(s["x1_ready"], 1)

            def stats2(b, u, h):
                dve.wait_ge(s["x1_ready"], b + 1)
                V_.bn_stats(at(ST, b), at(X, b)).then_inc(s["row_stats"], 1)
            steps(dve, NB, [(last_head, 0), (add_heads, 2), (stats2, 3)])
            dve.wait_ge(s["row_stats"], NB)
            moments(2, NB, D)

            def global_max(k, n):
                dve.wait_ge(s["gmT"], k + 1)
                link(V_.tensor_reduce(gr[0:n, 1:2], ps[5 if k == 3 else 0][0:n, 0:P], AX.X, ALU.max))
                V_.tensor_scalar(gd[0:n, 0:n], ident[0:n, 0:n], gr[0:n, 1:2], None, ALU.mult).then_inc(s["gr_ready"], 1)
                dve.wait_ge(s["gm_all"], k + 1)

            def xl(b, u, h):
                normed(at(XL, b), b).then_inc(s["xl_ready"], 1)

            def xl_max(b, u, h):
                dve.wait_ge(s["xl_ready"], b + 1)
                V_.tensor_reduce(am[:, 0, cols(b, 1)], at(XL, b), AX.X, ALU.max, apply_absolute_value=True).then_inc(s["xl_max"], 1)
            steps(dve, NB, [(xl, 0), (xl_max, 1)])
            dve.wait_ge(s["xl_max"], NB)
            V_.tensor_reduce(gm[:, 0:1], am[:, 0, 0:NB], AX.X, ALU.max).then_inc(s["gm_ready"], 1)
            global_max(0, 1)
            link(V_.tensor_scalar(sc[:, 0:1], ps[0][:, 256:257], 1.0 / QMAX, TINY, ALU.mult, ALU.max))
            link(V_.reciprocal(sc[:, 1:2], sc[:, 0:1]))

            def x_int(b, u):
                V_.tensor_scalar(at(XL, b), at(XL, b), sc[:, 1:2], ROUND, ALU.mult, ALU.add).then_inc(s["offset"], 1)
                dve.wait_ge(s["offset"], b + 1)
                free_after(dve, s["tr3_done"], b)
                V_.tensor_scalar(T[:, u, :], at(XL, b), -ROUND, QMAX, ALU.add, ALU.min).then_inc(s["xi_ready"], 1)

            def piece_max(t, name, c, f):
                dve.wait_ge(s[f"{name}_out"], c * FT + f + 1)
                V_.tensor_reduce(am[:, 0 if name == "gate" else 1, cols(c * FT + f, 1)], t[:, f, cols(c, 512)], AX.X, ALU.max,
                                 apply_absolute_value=True).then_inc(s[f"{name}_max"], 1)

            def gate_chunk(c):
                for f in range(FT):
                    if f < 4 and not (isinstance(c, int) and c == 3):
                        x_int(4 * c + 4 + f, f % 2)
                    piece_max(G, "gate", c, f)
            for j in range(4):
                x_int(j, j % 2)
            gate_chunk(0)
            with dve.Fori(1, 3) as c:
                gate_chunk(c)
            gate_chunk(3)
            dve.wait_ge(s["gate_max"], 4 * FT)
            V_.tensor_reduce(gm[:, 0:1], am[:, 0, :], AX.X, ALU.max).then_inc(s["gm_ready"], 1)
            global_max(1, 1)
            link(V_.tensor_scalar(sc[:, 3:4], ps[0][:, 256:257], sc[:, 0:1], None, ALU.mult))
            link(V_.tensor_scalar(sc[:, 5:6], sc[:, 3:4], 1.0 / QMAX, TINY, ALU.mult, ALU.max))
            link(V_.reciprocal(sc[:, 9:10], sc[:, 5:6]))
            link(V_.tensor_scalar(sc[:, 7:8], sc[:, 9:10], sc[:, 0:1], None, ALU.mult))
            V_.tensor_scalar(sc[:, 14:15], sc[:, 5:6], 1.0 / 65536.0, None, ALU.mult).then_inc(s["sc_gate"], 1)

            def g_to_int(b, u):
                free_after(dve, s["gs_done"], b)
                V_.tensor_scalar(GI[:, u], F_b(G, b), sc[:, 7:8], None, ALU.mult).then_inc(s["g_int1"], 1)

            def gate_sig(b, u):
                dve.wait_ge(s["sig_int"], b + 1)
                V_.tensor_tensor(F_b(G, b), GI[:, u], SI[:, u], ALU.mult).then_inc(s["gs_done"], 1)

            def gs_max(b):
                dve.wait_ge(s["gs_done"], b + 1)
                V_.tensor_reduce(am[:, 0, cols(b, 1)], F_b(G, b), AX.XY, ALU.max, apply_absolute_value=True).then_inc(s["gs_max"], 1)

            def up_chunk(c):
                for j in range(4):
                    if j % 2 == 0:
                        g_to_int(4 * c + j + 1, 1)
                    gate_sig(4 * c + j, j % 2)
                    if not (isinstance(c, int) and c == 0 and j < 1):
                        gs_max(4 * c + j - 1)
                    piece_max(U, "up", c, j)
                piece_max(U, "up", c, 4)
                piece_max(U, "up", c, 5)
            up_chunk(0)
            with dve.Fori(1, 4) as c:
                up_chunk(c)
            gs_max(NB - 1)
            dve.wait_ge(s["gs_max"], NB)
            V_.tensor_reduce(gm[:, 0:1], am[:, 0, 0:NB], AX.X, ALU.max)
            V_.tensor_reduce(gm[:, 1:2], am[:, 1, :], AX.X, ALU.max).then_inc(s["gm_ready"], 1)
            global_max(2, 2)
            gs_all, up_all = ps[0][:, 256:257], ps[0][:, 257:258]
            link(V_.tensor_scalar(sc[:, 15:16], gs_all, sc[:, 14:15], 1.0 / QMAX, ALU.mult, ALU.mult))
            link(V_.tensor_scalar(sc[:, 2:3], up_all, sc[:, 0:1], 1.0 / QMAX, ALU.mult, ALU.mult))
            link(V_.tensor_scalar(sc[:, 15:16], sc[:, 15:16], TINY, None, ALU.max))
            link(V_.tensor_scalar(sc[:, 4:5], sc[:, 2:3], TINY, None, ALU.max))
            link(V_.reciprocal(sc[:, 16:17], sc[:, 15:16]))
            link(V_.reciprocal(sc[:, 8:9], sc[:, 4:5]))
            link(V_.tensor_scalar(sc[:, 10:11], sc[:, 16:17], sc[:, 14:15], None, ALU.mult))
            V_.tensor_scalar(sc[:, 6:7], sc[:, 8:9], sc[:, 0:1], None, ALU.mult).then_inc(s["sc_up"], 1)

            def g2_int(b, u, h):
                free_after(dve, s["prod"], b)
                V_.tensor_scalar(G2[:, u], F_b(G, b), sc[:, 10:11], None, ALU.mult).then_inc(s["g2_int"], 1)

            def product(b, u, h):
                dve.wait_ge(s["g2_int"], b + 1)
                dve.wait_ge(s["u_int"], b + 1)
                V_.tensor_tensor(F_b(U, b), UI[:, u], G2[:, u], ALU.mult).then_inc(s["prod"], 1)

            def product_max(b, u, h):
                dve.wait_ge(s["prod"], b + 1)
                V_.tensor_reduce(am[:, 0, cols(b, 1)], F_b(U, b), AX.XY, ALU.max, apply_absolute_value=True).then_inc(s["prod_max"], 1)
            steps(dve, NB, [(g2_int, 0), (product_max, 2), (product, 1)])
            dve.wait_ge(s["prod_max"], NB)
            V_.tensor_reduce(gm[:, 0:1], am[:, 0, 0:NB], AX.X, ALU.max).then_inc(s["gm_ready"], 1)
            global_max(3, 1)
            link(V_.tensor_scalar(sc[:, 17:18], sc[:, 15:16], sc[:, 4:5], None, ALU.mult))
            link(V_.tensor_scalar(sc[:, 18:19], ps[5][:, 256:257], sc[:, 17:18], 1.0 / QMAX, ALU.mult, ALU.mult))
            link(V_.tensor_scalar(sc[:, 18:19], sc[:, 18:19], TINY, None, ALU.max))
            link(V_.reciprocal(sc[:, 19:20], sc[:, 18:19]))
            link(V_.tensor_scalar(sc[:, 13:14], sc[:, 19:20], sc[:, 17:18], None, ALU.mult))

            def o_int(b, u, h):
                V_.tensor_scalar(F_b(U, b), F_b(U, b), sc[:, 13:14], ROUND, ALU.mult, ALU.add).then_inc(s["offset"], 1)
                dve.wait_ge(s["offset"], NB + b + 1)
                free_after(dve, s["down_done"], b)
                V_.tensor_scalar(OT[:, u], F_b(U, b), -ROUND, QMAX, ALU.add, ALU.min).then_inc(s["oi_ready"], 1)

            def residual(b, u, h):
                dve.wait_ge(s["down_done"], b + 1)
                V_.scalar_tensor_tensor(out=at(X, b), in0=ps[6 + u][:, 0:D], scalar=sc[:, 18:19], in1=at(X, b), op0=ALU.mult, op1=ALU.add).then_inc(s["x2_ready"], 1)

            def stats3(b, u, h):
                dve.wait_ge(s["x2_ready"], b + 1)
                V_.bn_stats(at(ST, b), at(X, b)).then_inc(s["row_stats"], 1)
            steps(dve, NB, [(o_int, 0), (residual, 1), (stats3, 2)])
            dve.wait_ge(s["row_stats"], 2 * NB)
            V_.tensor_scalar(bq[:, :], bq[:, :], 0.25, None, ALU.mult)
            moments(3, NB, D)

            def add_attn(b, u, h):
                dve.wait_ge(s["o_done"], b + 1)
                dve.wait_ge(s["bo_added"], b + 1)
                V_.tensor_tensor(at(X, b), ps[4][:, 2 * P:4 * P], at(X, b), ALU.add).then_inc(s["x3_ready"], 1)

            def stats4(b, u, h):
                dve.wait_ge(s["x3_ready"], b + 1)
                V_.bn_stats(at(ST, b), at(X, b)).then_inc(s["row_stats"], 1)

            def norm3(b, u, h):
                free_after(dve, s["c_tr"], b)
                normed(T[:, u, :], b).then_inc(s["xn3"], 1)

            def attn_out(b, u, h):
                dve.wait_ge(s["pv_done"], b + 1)
                o = ps[5][:, 0:NH1 * (DH1 + 1)].rearrange("p (h d) -> p h d", h=NH1)
                V_.reciprocal(rs[:, u, :], o[:, :, DH1]).then_inc(s["rs_ready"], 1)
                dve.wait_ge(s["rs_ready"], b + 1)
                free_after(dve, s["a_tr"], b)
                for e in range(2):
                    last = V_.tensor_tensor(AO[:, u, :].rearrange("p (e j r d) -> p e j r d", e=2, j=4, r=2)[:, e], o.rearrange("p (j e r) d -> p e j r d", j=4, e=2)[:, e, :, :, 0:DH1],
                                            rs[:, u, :].rearrange("p (j e r) -> p e j r", j=4, e=2)[:, e].unsqueeze(3).broadcast_to([P, 4, 2, DH1]), ALU.mult)
                last.then_inc(s["ao_ready"], 1)

            def softmax(b, u, h):
                dve.wait_ge(s["scores"], b + 1)
                sco = pA[:, :, :].rearrange("p j (k n) -> p (j k) n", n=P)
                V_.tensor_reduce(rm[:, u, :], sco, AX.X, ALU.max).then_inc(s["rm_ready"], 1)
                dve.wait_ge(s["rm_ready"], b + 1)
                free_after(dve, s["pv_done"], b)
                for e in range(2):
                    part = slice(e * NH1 // 2, (e + 1) * NH1 // 2)
                    V_.tensor_tensor(PR[:, u, part], sco[:, part], rm[:, u, part].unsqueeze(2).broadcast_to([P, NH1 // 2, P]), ALU.subtract).then_inc(s["s_sub"], 1)
            steps(dve, NB, [(softmax, 2), (norm3, 0), (add_attn, 4), (attn_out, 3), (stats4, 4)])
            dve.wait_ge(s["row_stats"], 3 * NB)
            moments(4, NB, D)

            def norm4(c, u, h):
                free_after(dve, s["d_tr"], c)
                for j in range(2):
                    last = normed((T, Cu)[u][:, j, :], 2 * c + j)
                last.then_inc(s["xn4"], 1)
                for j in range(2):
                    last = normed(at(XR, 2 * c + j)[:, 0:D], 2 * c + j)
                last.then_inc(s["xr_ready"], 1)
            steps(dve, NB // 2, [(norm4, 0)])
            dve.wait_ge(s["tables"], 1)
            V_.tensor_copy(cidx[:, :], cidx_f)
            V_.tensor_copy(ids[:, 0:2 * NB].rearrange("p (b c) -> p b c", b=NB), ids_f)
            dve.wait_ge(s["d_lg"], NB // 2)
            logits = ps[2][:, 0:NB * NE].rearrange("p (b e) -> p b e", b=NB)

            def per_e(ap):
                return ap.unsqueeze(2).broadcast_to([P, NB, NE])
            link(V_.tensor_reduce(r1[:, :], logits, AX.X, ALU.max))
            V_.tensor_tensor(LG[:, :, :], logits, per_e(r1[:, :]), ALU.subtract).then_inc(s["lg_sub"], 1)
            dve.wait_ge(s["lg_exp"], 1)
            link(V_.tensor_reduce(r1[:, :], LG[:, :, :], AX.X, ALU.add))
            link(V_.reciprocal(r1[:, :], r1[:, :]))
            V_.tensor_tensor(LW[:, :, :], LG[:, :, :], per_e(r1[:, :]), ALU.mult)
            V_.tensor_tensor(LG[:, :, :], LG[:, :, :], per_e(r1[:, :]), ALU.mult).then_inc(s["probs"], 1)
            dve.wait_ge(s["probs"], 1)
            for k in range(TOPK):
                link(V_.tensor_reduce(gates[:, k, :], LW[:, :, :], AX.X, ALU.max))
                link(V_.tensor_tensor(q1[:, :, :], LW[:, :, :], per_e(gates[:, k, :]), ALU.is_equal))
                link(V_.tensor_tensor(q1[:, :, :], q1[:, :, :], rank8[:, :, :], ALU.mult))
                link(V_.tensor_reduce(r1[:, :], q1[:, :, :], AX.X, ALU.max))
                link(V_.tensor_tensor(OH[:, k], q1[:, :, :], per_e(r1[:, :]), ALU.is_equal))
                if k + 1 < TOPK:
                    link(V_.scalar_tensor_tensor(out=LW[:, :, :], in0=OH[:, k], scalar=-2.0, in1=LW[:, :, :], op0=ALU.mult, op1=ALU.add))
            V_.tensor_copy(OHb[:, :], OH[:, :, :, :].rearrange("p k b e -> p (k b e)")).then_inc(s["oh_ready"], 1)
            dve.wait_ge(s["cnt_done"], 1)
            for g in range(NG):
                for k in range(TOPK):
                    last = V_.tensor_copy(tot[:, g, :, k, :], ps[5][:, 0:TOPK * NB * NE].rearrange("p (k g t e) -> p k g e t", k=TOPK, g=NG, t=TG)[:, k, g])
            link(last)
            link(V_.tensor_tensor_scan(inc[:, :, :, :, :].rearrange("p g e k t -> p (g e k t)"), segm[:, :],
                                       tot[:, :, :, :, :].rearrange("p g e k t -> p (g e k t)"), 0.0, ALU.mult, ALU.add))
            link(V_.tensor_tensor(inc[:, :, :, :, :].rearrange("p g e k t -> p (g e k t)"), inc[:, :, :, :, :].rearrange("p g e k t -> p (g e k t)"),
                                  tot[:, :, :, :, :].rearrange("p g e k t -> p (g e k t)"), ALU.subtract))
            for g in range(NG):
                for k in range(TOPK):
                    last = V_.tensor_tensor(pos[:, k, g * TG:(g + 1) * TG, :],
                                            ps[4][:, 0:TOPK * NB * NE].rearrange("p (k g t e) -> p k g t e", k=TOPK, g=NG, t=TG)[:, k, g],
                                            inc[:, g, :, k, :].rearrange("p e t -> p t e"), ALU.add)
            link(last)
            link(V_.scalar_tensor_tensor(out=tmp[:, :, :, :], in0=pos[:, :, :, :], scalar=1.0, in1=OH[:, :, :, :], op0=ALU.add, op1=ALU.mult))
            link(V_.tensor_tensor(place[:, :, :], tmp[:, 0], tmp[:, 1], ALU.add))
            V_.tensor_scalar(shift[:, :, :], place[:, :, :], CAP + 1.0, 4.0 * SELW, ALU.is_ge, ALU.mult)
            link(V_.tensor_scalar(q1[:, TG:, :], place[:, TG:, :], P + 1.0, float(SPARE), ALU.is_ge, ALU.mult))
            link(V_.tensor_tensor(place[:, :, :], place[:, :, :], shift[:, :, :], ALU.add))
            link(V_.tensor_tensor(place[:, TG:, :], place[:, TG:, :], q1[:, TG:, :], ALU.add))
            link(V_.tensor_copy(placeb[:, :, :], place[:, :, :]))

            def select(e, u, h):
                free_after(dve, s["id_done"], e)
                V_.tensor_tensor(SEL[:, u], placeb[:, :, cols(e, 1)].broadcast_to([P, NB, SELW]),
                                 cidx[:, :].unsqueeze(1).broadcast_to([P, NB, SELW]), ALU.is_equal).then_inc(s["sel_ready"], 1)

            def number(e, u, h):
                dve.wait_ge(s["id_done"], e + 1)
                chunks = ((P, 0, 2), (ROWS - 2 * P, 2, 3))
                for n, c, c1 in chunks:
                    last = V_.tensor_reduce(num[0:n, u, c:c1], ps[7][0:n, 2 * c:2 * c1].rearrange("p (c i) -> p c i", i=2), AX.X, ALU.add)
                last.then_inc(s["num_ready"], 1)
                dve.wait_ge(s["num_ready"], e + 1)
                for n, c, c1 in chunks:
                    last = V_.tensor_scalar(token[0:n, cols(e, 1), c:c1].squeeze(1), num[0:n, u, c:c1], float(NB * S), None, ALU.add)
                last.then_inc(s["token_ready"], 1)

            def gate_column(e, u, h):
                dve.wait_ge(s[f"xe_in{u}"], 48 * (h + 1))
                free_after(dve, s["y_ready"], e, 3)
                V_.tensor_copy(gcol[:, u, :], XE[:, u, :, bass.ds(D + e, 1)].squeeze(2)).then_inc(s["gcol_ready"], 1)

            def add_rows(e, u, h):
                dve.wait_ge(s["yg_in"], 48 * (e + 1))
                dve.wait_ge(s["gcol_ready"], e + 1)
                for c in range(3):
                    n = P if c < 2 else ROWS - 2 * P
                    dve.wait_ge(s["ec_done"], e * 3 + c + 1)
                    V_.scalar_tensor_tensor(out=YG[0:n, c, :], in0=ps[4 + c][0:n, 0:D], scalar=gcol[0:n, u, c:c + 1], in1=YG[0:n, c, :],
                                            op0=ALU.mult, op1=ALU.add).then_inc(s["y_ready"], 1)
            steps(dve, NE, [(number, 1), (select, 0), (add_rows, 4), (gate_column, 2)])

        @block.tensor
        def _(pe):
            mm, tr = nc.tensor.matmul, nc.tensor.transpose
            pe.wait_ge(s["consts"], 1)
            def ctx_cols(u, k):
                return Cu[:, u, k * P:(k + 1) * P]

            def turn(b, u, h):
                pe.wait_ge(s["xln_ready"], b + 1)
                free_after(pe, s["xct_ready"], b)
                for k in range(KD):
                    tr(ps[u][:, k * P:(k + 1) * P], T[:, u, k * P:(k + 1) * P], ident[:, :])
                for k in range(KD):
                    last = tr(ps[u][:, (2 + k) * P:(3 + k) * P], ctx_cols(u, k), ident[:, :])
                last.then_inc(s["tr_done"], 1)

            def gates(b, u, h):
                pe.wait_ge(s["xct_ready"], b + 1)
                for k in range(4):
                    last = mm(ps[6][:, bass.ds(b * 2 * NH0, P)], XCT[:, u, k, :], wgate_f[:, k * 2 * NH0:k * 2 * NH0 + P], start=(k == 0), stop=(k == 3))
                last.then_inc(s["g_done"], 1)
            pe.wait_ge(s["gw_ready"], 1)
            steps(pe, NB, [(turn, 0), (gates, 1)])

            pe.wait_ge(s["fgate_dve"], 2)
            mm(ps[7][:, 256:256 + NB * NH0], tri[:, :], lf[:, :, :].rearrange("p b h -> p (b h)"), start=True, stop=True).then_inc(s["fgate_pe"], 1)
            pe.wait_ge(s["fgate_dve"], 3)
            tr(ps[7][0:NB * NH0, 0:P], Acol[:, :, :].rearrange("p b h -> p (b h)"), ident[:, :]).then_inc(s["fgate_pe"], 1)
            pe.wait_ge(s["fgate_dve"], 4)
            tr(ps[7][:, P:P + NB * NH0], mT[:, :], ident[0:NB * NH0, 0:NB * NH0]).then_inc(s["fgate_pe"], 1)

            def turn2(b, u, h):
                pe.wait_ge(s["xln2_ready"], b + 1)
                free_after(pe, s["c_copied"], b)
                for k in range(KD):
                    tr(ps[u][:, k * P:(k + 1) * P], T[:, u, k * P:(k + 1) * P], ident[:, :])
                for k in range(KD):
                    last = tr(ps[u][:, (2 + k) * P:(3 + k) * P], ctx_cols(u, k), ident[:, :])
                last.then_inc(s["tr2_done"], 1)

            def spread_max(b, u, h):
                free_after(pe, s["decay"], b)
                for n in range(NH0):
                    last = tr(ps[2 + u][:, n * P:(n + 1) * P], MAu[:, u, n:n + 1].broadcast_to([P, P]), ident[:, :])
                last.then_inc(s["mb_done"], 1)

            def scores0(b, u, h):
                pe.wait_ge(s["c_copied"], b + 1)
                if not (isinstance(b, int) and b < 1):
                    pe.wait_ge(s["c_ready"], b)
                for n in range(NH0):
                    r = DH0 * (n % 2)
                    last = mm(pB[:, n % 2, (n // 2) * P:(n // 2 + 1) * P], XCT[r:r + DH0, u, 2 + n // 2, :], XCT[r:r + DH0, u, n // 2, :], start=True, stop=True)
                last.then_inc(s["qk_done"], 1)

            def values0(b, u, h):
                pe.wait_ge(s["c_masked"], b + 1)
                pe.wait_ge(s["v_copied"], b + 1)
                free_after(pe, s["u_copied"], b)
                if isinstance(b, int) and b == 0:
                    pe.wait_ge(s["fgate_dve"], 5)
                w = DH0 + 1
                for n in range(NH0):
                    last = mm(pC[:, u, n * w:n * w + P], HC[:, u, 2 * (n % 2) + n // 2, :], VUf[:, u, n * w:n * w + P], start=True, stop=True)
                last.then_inc(s["av_done"], 1)
            steps(pe, NB, [(turn2, 0), (spread_max, 0), (scores0, 1), (values0, 2)])

            pe.wait_ge(s["decay"], NB)
            pe.wait_ge(s["w_q"], 2 * NB // 3 + 1)
            for n in range(13):
                if n == 6:
                    pe.wait_ge(s["w_q"], NB)
                if n >= 2:
                    pe.wait_ge(s["wtr_copied"], n - 1)
                if n >= 9:
                    pe.wait_ge(s[f"w{'qkvo'[n - 9]}_in"], 16)
                for k in range(2):
                    for c in range(2):
                        if n < 6:
                            src = WN[:, n // 3, (2 * (n % 3) + c) * D + k * P:(2 * (n % 3) + c) * D + (k + 1) * P]
                        elif n < 9:
                            src = WN[:, 2, c * FF + (2 * (n - 6) + k) * P:c * FF + (2 * (n - 6) + k + 1) * P]
                        else:
                            src = LN[:, n - 9, c, k * P:(k + 1) * P]
                        last = tr(ps[2 + n % 2][:, (2 * k + c) * P:(2 * k + c + 1) * P], src, ident[:, :])
                last.then_inc(s["wtr_done"], 1)

            def whole_max(k, n):
                pe.wait_ge(s["gm_ready"], k + 1)
                bank = ps[5 if k == 3 else 0]
                tr(bank[0:n, 0:P], gm[:, 0:n], ident[:, :]).then_inc(s["gmT"], 1)
                pe.wait_ge(s["gr_ready"], k + 1)
                mm(bank[:, 256:256 + n], ones[0:n, :], gd[0:n, 0:n], start=True, stop=True).then_inc(s["gm_all"], 1)

            pe.wait_ge(s["wtr_copied"], 13)
            pe.wait_ge(s["u_copied"], NB)
            whole_max(0, 1)

            def turn3(b, u):
                pe.wait_ge(s["xi_ready"], b + 1)
                free_after(pe, s["xit_ready"], b)
                for k in range(KD):
                    last = tr(ps[u][:, k * P:(k + 1) * P], T[:, u, k * P:(k + 1) * P], ident[:, :])
                last.then_inc(s["tr3_done"], 1)

            def product(w, name, c, f):
                for k in range(KD):
                    last = mm(ps[2 + f][:, :], w[:, k, f * P:(f + 1) * P], XITv[:, k, cols(c, 512)], start=(k == 0), stop=(k == KD - 1))
                last.then_inc(s[f"{name}_done"], 1)

            def gate_chunk(c):
                pe.wait_ge(s["xit_ready"], 4 * c + 4)
                for f in range(FT):
                    if not (isinstance(c, int) and c == 0):
                        pe.wait_ge(s["gate_out"], (c - 1) * FT + f + 1)
                    product(wgtT, "gate", c, f)
                    if f < 4 and not (isinstance(c, int) and c == 3):
                        turn3(4 * c + 4 + f, f % 2)
            for j in range(4):
                turn3(j, j % 2)
            gate_chunk(0)
            with pe.Fori(1, 3) as c:
                gate_chunk(c)
            gate_chunk(3)

            def up_chunk(c):
                for f in range(FT):
                    if isinstance(c, int):
                        pe.wait_ge(s["gate_out"], 3 * FT + f + 1)
                    else:
                        pe.wait_ge(s["up_out"], (c - 1) * FT + f + 1)
                    product(wupT, "up", c, f)
            whole_max(1, 1)
            up_chunk(0)
            with pe.Fori(1, 4) as c:
                up_chunk(c)
            whole_max(2, 2)

            def turn4(b, u, h):
                pe.wait_ge(s[f"ctx_in{u}"], (h + 1) * 16)
                if isinstance(b, int) and b == 0:
                    pe.wait_ge(s["sc_up"], 1)
                free_after(pe, s["xct4_ready"], b)
                for k in range(KD):
                    last = tr(ps[u][:, k * P:(k + 1) * P], ctx_cols(u, k), ident[:, :])
                last.then_inc(s["tr4_done"], 1)

            def project(b, u, h):
                pe.wait_ge(s["xct4_ready"], b + 1)
                free_after(pe, s["kv_copied"], b)
                for e in range(KD):
                    for k in range(KD):
                        mm(ps[2 + u][:, e * P:(e + 1) * P], wT[1][:, k, e * P:(e + 1) * P], XCT[:, u, 2 + k, :], start=(k == 0), stop=(k == KD - 1))
                for k in range(KD):
                    last = mm(ps[2 + u][:, 2 * P:4 * P], XCT[:, u, 2 + k, :], wT[2][:, k, :], start=(k == 0), stop=(k == KD - 1))
                last.then_inc(s["kv_done"], 1)
            pe.wait_ge(s["up_out"], 4 * FT)
            steps(pe, NB, [(turn4, 0), (project, 1)])
            whole_max(3, 1)

            def down(b, u, h):
                pe.wait_ge(s["oi_ready"], b + 1)
                free_after(pe, s["x2_ready"], b)
                for f in range(FT):
                    last = mm(ps[6 + u][:, 0:D], OT[:, u, f, :], wdnT[:, f, :], start=(f == 0), stop=(f == FT - 1))
                last.then_inc(s["down_done"], 1)
            steps(pe, NB, [(down, 0)])

            def c_turn(b, u, h):
                pe.wait_ge(s["xn3"], b + 1)
                if isinstance(b, int) and b < 4:
                    if b >= 1:
                        pe.wait_ge(s["qt_ready"], b)
                else:
                    pe.wait_ge(s["x3_ready"], b - 3)
                for k in range(KD):
                    last = tr(ps[4][:, k * P:(k + 1) * P], T[:, u, k * P:(k + 1) * P], ident[:, :])
                last.then_inc(s["c_tr"], 1)

            def c_query(b, u, h):
                pe.wait_ge(s["c_xt"], b + 1)
                for e in range(KD):
                    for k in range(KD):
                        last = mm(ps[4][:, (2 + e) * P:(3 + e) * P], wT[0][:, k, e * P:(e + 1) * P], XCT[:, u, k, :], start=(k == 0), stop=(k == KD - 1))
                last.then_inc(s["c_q"], 1)

            def c_scores(b, u, e):
                for j in range(4):
                    last = mm(ps[j][:, 2 * e * P:(2 * e + 2) * P], QT[32 * j:32 * j + 32, u, e, :],
                              KM[32 * j:32 * j + 32, u, e, :, :].rearrange("p r n -> p (r n)"), start=True, stop=True)
                return last

            def scores_first(b, u, h):
                pe.wait_ge(s["qt_ready"], b + 1)
                pe.wait_ge(s["km_ready"], b + 1)
                if not (isinstance(b, int) and b < 1):
                    pe.wait_ge(s["s_sub"], 2 * b)
                c_scores(b, u, 0)

            def scores_rest(b, u, h):
                c_scores(b, u, 1).then_inc(s["scores"], 1)

            def turn_group(b, u, g):
                if not (isinstance(b, int) and 4 * b + g < 2):
                    pe.wait_ge(s["pt_ready"], 4 * b + g - 1)
                for n in range(4):
                    last = tr(pC[:, g % 2, n * P:(n + 1) * P], PR[:, u, 4 * g + n, :], ident[:, :])
                last.then_inc(s["pt_tr"], 1)

            def value_group(b, u, g):
                w = DH1 + 1
                pe.wait_ge(s["pt_ready"], 4 * b + g + 1)
                for n in range(4):
                    head = 8 * (n // 2) + 2 * g + n % 2
                    last = mm(ps[5][:, (4 * g + n) * w:(4 * g + n) * w + WIDE], PT[:, u, 4 * g + n, :], Vf[:, bass.ds(b * VW + head * w, WIDE)], start=True, stop=True)
                return last

            def turn_first(b, u, h):
                pe.wait_ge(s["p_ready"], 2 * b + 1)
                turn_group(b, u, 0)
                turn_group(b, u, 1)

            def values_first(b, u, h):
                if not (isinstance(b, int) and b < 1):
                    pe.wait_ge(s["ao_ready"], b)
                value_group(b, u, 0)
                pe.wait_ge(s["p_ready"], 2 * b + 2)
                turn_group(b, u, 2)
                value_group(b, u, 1)
                turn_group(b, u, 3)

            def values_third(b, u, h):
                value_group(b, u, 2)

            def values_last(b, u, h):
                value_group(b, u, 3).then_inc(s["pv_done"], 1)

            def a_turn(b, u, h):
                pe.wait_ge(s["ao_ready"], b + 1)
                if isinstance(b, int) and b + 3 >= NB:
                    pe.wait_ge(s["x3_ready"], b)
                else:
                    pe.wait_ge(s["qt_ready"], b + 4)
                for k in range(KD):
                    last = tr(ps[4][:, k * P:(k + 1) * P], AO[:, u, k * P:(k + 1) * P], ident[:, :])
                last.then_inc(s["a_tr"], 1)

            def a_out(b, u, h):
                pe.wait_ge(s["at_ready"], b + 1)
                for k in range(KD):
                    last = mm(ps[4][:, 2 * P:4 * P], AT[:, u, k, :], wT[3][:, k, :], start=(k == 0), stop=(k == KD - 1))
                last.then_inc(s["o_done"], 1)
            steps(pe, NB, [(scores_first, 1), (c_turn, 0), (turn_first, 2), (scores_rest, 1), (c_query, 0), (values_first, 2),
                           (a_turn, 3), (values_third, 2), (a_out, 3), (values_last, 2)])

            def d_turn(c, u, h):
                pe.wait_ge(s["xn4"], c + 1)
                free_after(pe, s["d_xt"], c)
                for j in range(2):
                    for k in range(KD):
                        last = tr(ps[u][:, (2 * j + k) * P:(2 * j + k + 1) * P], (T, Cu)[u][:, j, k * P:(k + 1) * P], ident[:, :])
                last.then_inc(s["d_tr"], 1)

            def d_logits(c, u, h):
                pe.wait_ge(s["d_xt"], c + 1)
                for j in range(2):
                    for k in range(KD):
                        last = mm(ps[2][:, bass.ds((2 * c + j) * NE, P)], XCT[:, u, 2 * j + k, :], wrt_f[:, k * NE:k * NE + P], start=(k == 0), stop=(k == KD - 1))
                last.then_inc(s["d_lg"], 1)
            steps(pe, NB // 2, [(d_turn, 0), (d_logits, 1)])
            pe.wait_ge(s["oh_ready"], 1)
            mm(ps[4][:, 0:TOPK * NB * NE], stri[:, :], OHb[:, :], start=True, stop=True)
            mm(ps[5][:, 0:TOPK * NB * NE], onesb[:, :], OHb[:, :], start=True, stop=True).then_inc(s["cnt_done"], 1)

            def e_tokens(e, u, h):
                pe.wait_ge(s["sel_ready"], e + 1)
                if not (isinstance(e, int) and e < 1):
                    pe.wait_ge(s["token_ready"], e)
                for c, tiles in ((0, range(TG)), (1, range(TG, NB)), (2, range(NB))):
                    n = P if c < 2 else ROWS - 2 * P
                    for b in tiles:
                        last = mm(ps[7][0:n, 2 * c:2 * c + WIDE], SEL[:, u, b, 0:P] if c < 2 else SEL[:, u, b, P:], ids[:, 2 * b:2 * b + WIDE],
                                  start=(b == tiles[0]), stop=(b == tiles[-1]))
                last.then_inc(s["id_done"], 1)

            def e_turn(e, u, h):
                pe.wait_ge(s[f"xe_in{u}"], (h + 1) * 48)
                if not (isinstance(e, int) and e < 1):
                    pe.wait_ge(s["xet_ready"], e)
                for k in range(KD):
                    for c in range(3):
                        n = P if c < 2 else ROWS - 2 * P
                        last = tr(ps[k][:, c * P:c * P + n], XE[0:n, u, c, k * P:(k + 1) * P], ident[0:n, 0:n])
                last.then_inc(s["xe_tr"], 1)

            def e_hidden(e, u, h):
                pe.wait_ge(s["xet_ready"], e + 1)
                pe.wait_ge(s[f"wi_in{u}"], (h + 1) * 16)
                for f in range(NFT):
                    if not (isinstance(e, int) and e * NFT + f < 2):
                        pe.wait_ge(s["h_relu"], e * NFT + f - 1)
                    for k in range(KD):
                        last = mm(ps[2 + f % 2][:, 0:ROWS], WI[:, u, k, f * P:(f + 1) * P], XET[:, u, k, :], start=(k == 0), stop=(k == KD - 1))
                    last.then_inc(s["h_done"], 1)

            def e_out(e, u, h):
                pe.wait_ge(s["h_relu"], (e + 1) * NFT)
                pe.wait_ge(s[f"wo_in{u}"], (h + 1) * 16)
                if not (isinstance(e, int) and e < 1):
                    pe.wait_ge(s["y_ready"], 3 * e)
                for c in range(3):
                    n = P if c < 2 else ROWS - 2 * P
                    for f in range(NFT):
                        last = mm(ps[4 + c][0:n, 0:D], HT[:, u, f, c * P:c * P + n], WO[:, u, f, :], start=(f == 0), stop=(f == NFT - 1))
                    last.then_inc(s["ec_done"], 1)
            steps(pe, NE, [(e_hidden, 2), (e_turn, 1), (e_tokens, 0), (e_out, 3)])


_INS = ["x", "ctx_1024", "L0_xattn_igate_kernel", "L0_xattn_igate_bias", "L0_xattn_fgate_kernel", "L0_xattn_fgate_bias",
        "L0_xattn_outnorm_scale", "L0_ffn_w_gate", "L0_ffn_w_up", "L0_ffn_w_down", "L1_xattn_w_q", "L1_xattn_b_q",
        "L1_xattn_w_k", "L1_xattn_b_k", "L1_xattn_w_v", "L1_xattn_b_v", "L1_xattn_w_o", "L1_xattn_b_o",
        "L1_ffn_w_router", "L1_ffn_wi", "L1_ffn_wo"]


def kernel(**inputs):
    import numpy as _np
    import concourse.bacc as _bacc
    from concourse import mybir as _mybir
    from concourse.bass_utils import run_bass_kernel_spmd as _run

    nc = _bacc.Bacc("TRN2", target_bir_lowering=False, num_devices=1)
    arrays, args = {}, {}
    for name in _INS:
        a = _np.ascontiguousarray(inputs[name])
        arrays[f"in_{name}"] = a
        args[name] = nc.dram_tensor(f"in_{name}", a.shape, _mybir.dt.from_np(a.dtype), kind="ExternalInput").ap()
    shape = tuple(arrays["in_x"].shape)
    out = nc.dram_tensor("out_0", shape, _mybir.dt.float32, kind="ExternalOutput").ap()
    build(nc, args, out)
    r = _run(nc, [arrays], core_ids=[0])
    return r.results[0]["out_0"]
```
